# Optimizing a Trainium2 kernel written in Bass

```python
import numpy as np
import jax
import jax.numpy as jnp

def _softmax(x, axis=-1):
    return jax.nn.softmax(x, axis=axis)

def _gelu(x):
    return jax.nn.gelu(x, approximate=True)

def _silu(x):
    return jax.nn.silu(x)

def _sigmoid(x):
    return jax.nn.sigmoid(x)

def _layernorm(x, axis=-1, eps=1e-05):
    m = jnp.mean(x, axis=axis, keepdims=True)
    v = jnp.var(x, axis=axis, keepdims=True)
    return (x - m) / jnp.sqrt(v + eps)

def _scatter_add(tgt, idx, src, axis=0):
    return tgt.at[idx].add(src)

def _segment_sum(src, seg, n):
    return jax.ops.segment_sum(src, seg, n)
kernel_name = 'mk_conv_preact_d4_conv_nchw16_r4_77368a'

def setup_inputs(seed: int=0):
    np.random.seed(seed)
    _w = jnp.asarray

    def _rec_inputs():
        import jax
        import jax.numpy as jnp
        _gk = jax.random.key(seed)
        x = -7.109e-05 + 0.9999 * jax.random.normal(jax.random.fold_in(_gk, 1), (8, 16, 128, 128), jnp.float32)
        return x
    x = _rec_inputs()

    def _L0_conv_setup():
        import jax, jax.numpy as jnp
        import numpy as np
        B, C_IN, H, W = (16, 16, 128, 128)
        C_OUT, KH, KW = (16, 3, 3)
        N_EXPERTS = 3
        key = jax.random.key(seed)
        k1, k2, k3, k4 = jax.random.split(key, 4)
        x = jax.random.normal(k1, (B, C_IN, H, W), dtype=jnp.float32)
        fan_in = C_IN * KH * KW
        bound = np.sqrt(6.0 / fan_in)
        w_experts = jax.random.uniform(k2, (N_EXPERTS, C_OUT, C_IN, KH, KW), minval=-bound, maxval=bound, dtype=jnp.float32)
        bias = jnp.zeros((C_OUT,), dtype=jnp.float32)
        fc_bound = 1.0 / np.sqrt(C_IN)
        fc_w = jax.random.uniform(k3, (N_EXPERTS, C_IN), minval=-fc_bound, maxval=fc_bound, dtype=jnp.float32)
        fc_b = jnp.zeros((N_EXPERTS,), dtype=jnp.float32)
        return {'x': x, 'w_experts': w_experts, 'bias': bias, 'fc_w': fc_w, 'fc_b': fc_b}
    _L0_conv_all = _L0_conv_setup()
    _L0_conv_in = {k: v for k, v in _L0_conv_all.items() if k in ('w_experts', 'bias', 'fc_w', 'fc_b')}
    del _L0_conv_all

    def _L1_conv_setup():
        import jax, jax.numpy as jnp
        import numpy as np
        _KERNEL_3x3 = np.array([[0.25, 0.25, 0.25], [0.25, 1.0, 0.25], [0.25, 0.25, 0.25]], dtype=np.float32)
        N, C, H, W = (8, 16, 256, 256)
        key = jax.random.key(seed)
        x = jax.random.normal(key, (N, C, H, W), dtype=jnp.float32)
        weight = jnp.broadcast_to(jnp.asarray(_KERNEL_3x3).reshape(1, 1, 3, 3), (C, 1, 3, 3))
        return {'x': x, 'weight': weight}
    _L1_conv_all = _L1_conv_setup()
    _L1_conv_in = {k: v for k, v in _L1_conv_all.items() if k in ('weight',)}
    del _L1_conv_all

    def _L2_conv_setup():
        import jax, jax.numpy as jnp
        import numpy as np
        from jax import lax
        DN = ('NCHW', 'OIHW', 'NCHW')
        key = jax.random.key(seed)
        x = jax.random.normal(key, (8, 16, 128, 128), dtype=jnp.float32)
        return {'x': x, 'r': 8}
    _L2_conv_all = _L2_conv_setup()
    _L2_conv_in = {k: v for k, v in _L2_conv_all.items() if k in ()}
    del _L2_conv_all

    def _L3_conv_setup():
        import jax, jax.numpy as jnp
        import numpy as np
        D_STATE = 8
        HIDDEN = 64

        def _neighbor_sum(x):
            B, C, H, W = x.shape
            xp = jnp.pad(x, ((0, 0), (0, 0), (1, 1), (1, 1)))
            full = sum((xp[:, :, di:di + H, dj:dj + W] for di in range(3) for dj in range(3)))
            return full - x
        key = jax.random.key(seed)
        ks = jax.random.split(key, 6)
        B, H, W = (4, 64, 64)
        c_in = 2 * D_STATE
        c_nbr = c_in * 8
        c_out = 8 * D_STATE
        s = 0.05
        return {'x_cat': jax.random.normal(ks[0], (B, c_in, H, W), dtype=jnp.float32), 'w1': jax.random.normal(ks[1], (HIDDEN, c_nbr), dtype=jnp.float32) * s, 'w2': jax.random.normal(ks[2], (HIDDEN, HIDDEN), dtype=jnp.float32) * s, 'w3': jax.random.normal(ks[3], (HIDDEN, HIDDEN), dtype=jnp.float32) * s, 'w4': jax.random.normal(ks[4], (HIDDEN, HIDDEN), dtype=jnp.float32) * s, 'w5': jax.random.normal(ks[5], (c_out, HIDDEN), dtype=jnp.float32) * s}
    _L3_conv_all = _L3_conv_setup()
    _L3_conv_in = {k: v for k, v in _L3_conv_all.items() if k in ('w1', 'w2', 'w3', 'w4', 'w5')}
    del _L3_conv_all
    return {'x': x, 'L0_conv_w_experts': _L0_conv_in['w_experts'], 'L0_conv_bias': _L0_conv_in['bias'], 'L0_conv_fc_w': _L0_conv_in['fc_w'], 'L0_conv_fc_b': _L0_conv_in['fc_b'], 'L1_conv_weight': _L1_conv_in['weight'], 'L3_conv_w1': _L3_conv_in['w1'], 'L3_conv_w2': _L3_conv_in['w2'], 'L3_conv_w3': _L3_conv_in['w3'], 'L3_conv_w4': _L3_conv_in['w4'], 'L3_conv_w5': _L3_conv_in['w5']}

def reference(x, L0_conv_w_experts, L0_conv_bias, L0_conv_fc_w, L0_conv_fc_b, L1_conv_weight, L3_conv_w1, L3_conv_w2, L3_conv_w3, L3_conv_w4, L3_conv_w5):
    import jax
    import jax.numpy as jnp

    def _L0_conv_ref(x, w_experts, bias, fc_w, fc_b):
        import jax, jax.numpy as jnp
        import numpy as np
        B, C_IN, H, W = (16, 16, 128, 128)
        C_OUT, KH, KW = (16, 3, 3)
        N_EXPERTS = 3
        pooled = x.mean(axis=(2, 3))
        routing = jax.nn.softmax(pooled @ fc_w.T + fc_b, axis=1)
        kernels = jnp.einsum('bn,noihw->boihw', routing, w_experts)
        xp = jnp.pad(x, ((0, 0), (0, 0), (1, 1), (1, 1)), mode='reflect')

        def conv_one(xi, ki):
            return jax.lax.conv_general_dilated(xi[None], ki, window_strides=(1, 1), padding='VALID', dimension_numbers=('NCHW', 'OIHW', 'NCHW'))[0]
        out = jax.vmap(conv_one)(xp, kernels)
        return out + bias[None, :, None, None]

    def _L1_conv_ref(x, weight):
        import jax, jax.numpy as jnp
        import numpy as np
        _KERNEL_3x3 = np.array([[0.25, 0.25, 0.25], [0.25, 1.0, 0.25], [0.25, 0.25, 0.25]], dtype=np.float32)
        N, C, H, W = (8, 16, 256, 256)
        c = x.shape[1]
        y = jnp.abs(x)
        out = jax.lax.conv_general_dilated(y, weight, window_strides=(1, 1), padding=((1, 1), (1, 1)), dimension_numbers=('NCHW', 'OIHW', 'NCHW'), feature_group_count=c)
        return out

    def _L2_conv_ref(x, r):
        import jax, jax.numpy as jnp
        import numpy as np
        from jax import lax
        DN = ('NCHW', 'OIHW', 'NCHW')
        C = x.shape[1]
        k = 2 * r + 1
        inv_k = jnp.asarray(1.0 / k, dtype=x.dtype)
        kx = jnp.full((C, 1, 1, k), inv_k, dtype=x.dtype)
        ky = jnp.full((C, 1, k, 1), inv_k, dtype=x.dtype)
        x = lax.conv_general_dilated(x, kx, window_strides=(1, 1), padding=[(0, 0), (r, r)], feature_group_count=C, dimension_numbers=DN)
        x = lax.conv_general_dilated(x, ky, window_strides=(1, 1), padding=[(r, r), (0, 0)], feature_group_count=C, dimension_numbers=DN)
        return x

    def _L3_conv_ref(x_cat, w1, w2, w3, w4, w5):
        import jax, jax.numpy as jnp
        import numpy as np
        D_STATE = 8
        HIDDEN = 64

        def _neighbor_sum(x):
            B, C, H, W = x.shape
            xp = jnp.pad(x, ((0, 0), (0, 0), (1, 1), (1, 1)))
            full = sum((xp[:, :, di:di + H, dj:dj + W] for di in range(3) for dj in range(3)))
            return full - x
        B, C, H, W = x_cat.shape
        d_state = C // 2
        nbr = _neighbor_sum(x_cat)
        xn = jnp.repeat(nbr, 8, axis=1)
        h = jax.nn.elu(jnp.einsum('bchw,oc->bohw', xn, w1))
        h = jax.nn.elu(jnp.einsum('bchw,oc->bohw', h, w2))
        h = jax.nn.elu(jnp.einsum('bchw,oc->bohw', h, w3))
        h = jax.nn.elu(jnp.einsum('bchw,oc->bohw', h, w4))
        F_int = jnp.einsum('bchw,oc->bohw', h, w5)
        d4 = 4 * d_state
        real = F_int[:, :d4].reshape(B, 4, d_state, H, W).mean(axis=1) * 0.1
        imag = F_int[:, d4:].reshape(B, 4, d_state, H, W).mean(axis=1) * 0.1
        return jnp.concatenate([real, imag], axis=1)

    def _gn(v, G=8, eps=1e-05):
        B_, C_, H_, W_ = v.shape
        g = v.reshape(B_, G, C_ // G, H_, W_)
        m = jnp.mean(g, axis=(2, 3, 4), keepdims=True)
        s = jnp.var(g, axis=(2, 3, 4), keepdims=True)
        return ((g - m) / jnp.sqrt(s + eps)).reshape(v.shape)

    def _ln_c(v, eps=1e-06):
        m = jnp.mean(v, axis=1, keepdims=True)
        s = jnp.var(v, axis=1, keepdims=True)
        return (v - m) / jnp.sqrt(s + eps)

    def _ln_t(v, eps=1e-05):
        m = jnp.mean(v, axis=-1, keepdims=True)
        s = jnp.var(v, axis=-1, keepdims=True)
        return (v - m) / jnp.sqrt(s + eps)

    def _to_tokens(v):
        B_, C_, H_, W_ = v.shape
        return v.reshape(B_, C_, H_ * W_).transpose(0, 2, 1)

    def _from_tokens(t, like):
        B_, C_, H_, W_ = like.shape
        return t.transpose(0, 2, 1).reshape(B_, C_, H_, W_)
    x = x + _L0_conv_ref(_gn(x), L0_conv_w_experts, L0_conv_bias, L0_conv_fc_w, L0_conv_fc_b)
    x = x + _L1_conv_ref(_gn(x), L1_conv_weight)
    x = x + _L2_conv_ref(_gn(x), 8)
    x = x + _L3_conv_ref(_gn(x), L3_conv_w1, L3_conv_w2, L3_conv_w3, L3_conv_w4, L3_conv_w5)
    return x

_drawn_inputs = setup_inputs


def setup_inputs(seed=0):
    import zlib

    import numpy as np

    out = dict(_drawn_inputs(seed))
    spreads = {'L0_conv_bias': (0.0, 0.1), 'L0_conv_fc_b': (0.0, 0.463)}
    factors = {'L0_conv_fc_w': 27.408,
     'L3_conv_w1': 8.0,
     'L3_conv_w2': 8.0,
     'L3_conv_w3': 8.0,
     'L3_conv_w4': 8.0,
     'L3_conv_w5': 8.0}
    for name, (base, spread) in spreads.items():
        noise = np.random.default_rng([zlib.crc32(name.encode()), seed]).standard_normal(out[name].shape)
        drawn = base * np.exp(spread * noise) if base else spread * noise
        out[name] = jnp.asarray(drawn.astype(out[name].dtype))
    for name, factor in factors.items():
        out[name] = (out[name] * factor).astype(out[name].dtype)
    return out
```

```python
from contextlib import ExitStack

import numpy as np

import concourse.bass as bass
from concourse import mybir

F32 = mybir.dt.float32
ALU = mybir.AluOpType
ACT = mybir.ActivationFunctionType
AX = mybir.AxisListType

B, C, H, W = 8, 16, 128, 128
R = 8
K = H // R
P = R * C
N = K * W
Q = 4
KB = K // Q
CH = KB * W
EXPERTS = 3
HID = 64
M = P // 32
BOX = 17
RAD = BOX // 2
PITCH = W + BOX
EPS = 1e-5
HALO = 6 * C
LAYERS = 4

CONSTS = {}


def _constants():
    r, c = np.divmod(np.arange(P), C)
    dr = r[None, :] - r[:, None]
    same = c[None, :] == c[:, None]
    parts = [("ident", np.eye(P)),
             ("group", (c[None, :] // 2 == c[:, None] // 2) / (2 * R)),
             ("neg_group", (c[None, :] // 2 == c[:, None] // 2) / (-2.0 * R)),
             ("chan", same / R)]
    for kh in range(3):
        parts.append((f"tap{kh}", same & (dr == 1 - kh)))
    parts += [("box_above", same & (dr <= 0)), ("box_own", same), ("box_below", same & (dr >= 0))]
    parts += [("near_own", same & (abs(dr) <= 1)),
              ("near_above", (same & (dr == 1 - R))[:, 0:32]),
              ("near_below", (same & (dr == R - 1))[:, P - 32:P])]
    hk = np.arange(P) % (2 * C)
    below, hc = np.divmod(hk, C)
    edge = np.where(below, R - 1, 0)[:, None]
    parts.append(("halo_tap", (hc[:, None] == c[None, :]) & (edge == r[None, :])))
    parts.append(("tap_mask", np.stack([np.arange(R)[None, :] == r[:, None] - kh + 1 for kh in range(3)], 1)))
    parts.append(("halo_mask", edge == np.arange(R)[None, :]))
    o = np.arange(P) % HID
    parts.append(("fold", (o // 32 * 8 + o % 8)[:, None] == np.arange(C)[None, :]))
    parts.append(("ones", np.ones((P, P))))
    parts.append(("neg_half", np.full((P, 1), -0.5)))
    at, cols = 0, []
    for name, m in parts:
        m = np.asarray(m, np.float32).reshape(P, -1)
        CONSTS[name] = (at, m.shape[1])
        cols.append(m)
        at += m.shape[1]
    return np.concatenate(cols, axis=1)


def build(nc, x, w_experts, conv_bias, fc_w, fc_b, w_depth, w1, w2, w3, w4, w5, consts, out):
    NCON = consts.shape[1]
    with ExitStack() as ctx:
        def sb(name, shape):
            return ctx.enter_context(nc.sbuf_tensor(name, shape, F32))

        def pb(name, shape):
            return ctx.enter_context(nc.psum_tensor(name, shape, F32))

        def sem(name):
            return ctx.enter_context(nc.semaphore(name))

        con = sb("con", [P, NCON])

        def const(name, rows=P):
            at, n = CONSTS[name]
            return con[0:rows, at:at + n]

        xs = sb("xs", [P, B * N])
        y0 = sb("y0", [P, K, W + 2])
        y1 = sb("y1", [P, K, W + 2])
        y2 = sb("y2", [P, K * PITCH + BOX])
        y3 = sb("y3", [P, K, W + 2])
        halo0 = sb("halo0", [HALO, K, W])
        halo1 = sb("halo1", [HALO, K, W])
        rowbox = sb("rowbox", [P, K + 2, PITCH])
        pairsum = sb("pairsum", [P, K, W])
        rownear = sb("rownear", [P, K + 2, W])
        near = sb("near", [P, N])
        u = sb("u", [P, 2, 2 * CH])
        g = sb("g", [P, 2, 2 * CH])

        wc = sb("wc", [P, EXPERTS, C, 9])
        wh = sb("wh", [HALO, EXPERTS, C])
        wmix = sb("wmix", [P, 2, C * 9])
        whmix = sb("whmix", [HALO, 2, C])
        t0 = sb("t0", [P, 3, P])
        tpart = sb("tpart", [P, 3, 3, P])
        th0 = sb("th0", [HALO, P])
        wd = sb("wd", [P, 9])
        wdh = sb("wdh", [HALO, 1])
        t1 = sb("t1", [P, 3, P])
        th1 = sb("th1", [HALO, P])
        bias0 = sb("bias0", [P, 1])
        fcT = sb("fcT", [C, EXPERTS])
        fcb = sb("fcb", [P, EXPERTS])

        w1raw = sb("w1raw", [P, P])
        w1eff = sb("w1eff", [P, C])
        wnat = sb("wnat", [P, M + 3, P])
        wT = sb("wT", [P, M + 3, P])
        w5raw = sb("w5raw", [HID, 2, HID])
        w5T = sb("w5T", [P, 32])
        s_row = sb("s_row", [P, 4])
        k_row = sb("k_row", [P, 4])

        bn = sb("bn", [P, Q, 6])
        ms = sb("ms", [P, 2])
        gs = sb("gs", [P, 4])
        nv = sb("nv", [P, 2])
        st = sb("st", [P, 2])
        pooled = sb("pooled", [C, 1])
        fcp = sb("fcp", [C, EXPERTS])
        logit = sb("logit", [P, EXPERTS])
        nmax = sb("nmax", [P, 1])
        ex = sb("ex", [P, EXPERTS + 1])
        route = sb("route", [P, EXPERTS])

        pz = pb("pz", [P, 2, 2 * CH])
        pc = pb("pc", [P, 2, CH])
        po = pb("po", [P, CH])
        psm = pb("psm", [P, 512])

        s_const = sem("s_const")
        s_weights = sem("s_weights")
        x_loaded = sem("x_loaded")
        zeroed = sem("zeroed")
        setup_dve = sem("setup_dve")
        setup_pe = sem("setup_pe")
        setup_pool = sem("setup_pool")
        stat_step = sem("stat_step")
        sums_mm = sem("sums_mm")
        norm_step = sem("norm_step")
        y0_written = sem("y0_written")
        y1_written = sem("y1_written")
        y2_written = sem("y2_written")
        y3_written = sem("y3_written")
        box_rows = sem("box_rows")
        near_rows = sem("near_rows")
        halo0_in = sem("halo0_in")
        halo1_in = sem("halo1_in")
        conv_mm = sem("conv_mm")
        conv_evac = sem("conv_evac")
        route_step = sem("route_step")
        logits_mm = sem("logits_mm")
        route_exp = sem("route_exp")
        mix_step = sem("mix_step")
        folded = sem("folded")
        z_mm = sem("z_mm")
        relu_done = sem("relu_done")
        exp_done = sem("exp_done")
        g_written = sem("g_written")
        out_mm = sem("out_mm")
        out_evac = sem("out_evac")
        out_stored = sem("out_stored")

        xv = x.rearrange("b c (k r) w -> b r c k w", r=R)
        ov = out.rearrange("b c (k r) w -> b r c k w", r=R)

        def sample(i, j=None):
            if j is None:
                return xs[:, bass.ds(i * N, N)]
            return xs[:, bass.ds(i * N + j * CH, CH)]

        def blocks(t, j):
            return t[:, j * KB:(j + 1) * KB, :]

        STAT = Q + 5
        NORM = 2
        ROUTE = 5
        MIX = 13
        HALO0 = 12 * 16
        HALO1 = 6 * 16
        LOAD = R * 16

        def zn(j, q, l, a):
            return j * (Q * LAYERS * 2) + (q * LAYERS + l) * 2 + a + 1

        block = ctx.enter_context(nc.Block())

        @block.sync
        def _(sp):
            NCONST_DMA = 1
            sp.dma_start(con[:, :], consts).then_inc(s_const, 16)

            def load(i):
                for r in range(R):
                    sp.dma_start(xs[r * C:(r + 1) * C, bass.ds(i * N, N)].rearrange("c (k w) -> c k w", w=W),
                                 xv[i, r] if isinstance(i, int) else xv[bass.ds(i, 1), r].rearrange("b c k w -> (b c) k w")
                                 ).then_inc(x_loaded, 16)

            load(0)
            wv = w_experts.rearrange("n o c a b -> c (n o) (a b)")
            for r in range(R):
                sp.dma_start(wc[r * C:(r + 1) * C, :, :, :].rearrange("c n o t -> c (n o) t"), wv).then_inc(s_weights, 16)
            dv = w_depth.rearrange("c z a b -> c (z a b)")
            for r in range(R):
                sp.dma_start(wd[r * C:(r + 1) * C, :], dv).then_inc(s_weights, 16)
            with nc.allow_non_contiguous_dma(reason="small weights, once"):
                for kw in range(3):
                    for below in range(2):
                        at = (kw * 2 + below) * C
                        tap = 2 * below * 3 + kw
                        sp.dma_start(wh[at:at + C, :, :].rearrange("c n o -> c (n o)"), wv[:, :, tap]).then_inc(s_weights, 16)
                        sp.dma_start(wdh[at:at + C, :], dv[:, tap:tap + 1]).then_inc(s_weights, 16)
                sp.dma_start(fcT[:, :], fc_w.rearrange("n c -> c n")).then_inc(s_weights, 16)
                for r in range(R):
                    sp.dma_start(bias0[r * C:(r + 1) * C, :], conv_bias.rearrange("(c z) -> c z", z=1)).then_inc(s_weights, 16)
                sp.dma_start(fcb[:, :], fc_b.rearrange("(z n) -> z n", z=1).to_broadcast([P, EXPERTS])).then_inc(s_weights, 16)
            for p in range(2):
                sp.dma_start(w1raw[p * HID:(p + 1) * HID, :], w1).then_inc(s_weights, 16)
                sp.dma_start(w5raw[:, p, :], w5).then_inc(s_weights, 16)
            sp.wait_ge(zeroed, 1)
            for p in range(2):
                for l, w in enumerate((w2, w3, w4)):
                    sp.dma_start(wnat[p * HID:(p + 1) * HID, M + l, p * HID:(p + 1) * HID], w).then_inc(s_weights, 16)

            def halos0(i):
                sp.wait_ge(y0_written, 3 * i + 3)
                for kw in range(3):
                    a, b = kw * 2 * C, (kw * 2 + 1) * C
                    for dst, rows in ((halo0[a:a + C, 1:K], y0[(R - 1) * C:P, 0:K - 1, kw:kw + W]),
                                      (halo0[a:a + C, 0:1], y0[C:2 * C, 0:1, kw:kw + W]),
                                      (halo0[b:b + C, 0:K - 1], y0[0:C, 1:K, kw:kw + W]),
                                      (halo0[b:b + C, K - 1:K], y0[(R - 2) * C:(R - 1) * C, K - 1:K, kw:kw + W])):
                        sp.dma_start(dst, rows).then_inc(halo0_in, 16)

            def halos1(i):
                sp.wait_ge(y1_written, i + 1)
                for kw in range(3):
                    a, b = kw * 2 * C, (kw * 2 + 1) * C
                    for dst, rows in ((halo1[a:a + C, 1:K], y1[(R - 1) * C:P, 0:K - 1, kw:kw + W]),
                                      (halo1[b:b + C, 0:K - 1], y1[0:C, 1:K, kw:kw + W])):
                        sp.dma_start(dst, rows).then_inc(halo1_in, 16)

            def store(j):
                sp.wait_ge(out_evac, Q * j + Q)
                for r in range(R):
                    sp.dma_start(ov[j, r] if isinstance(j, int) else ov[bass.ds(j, 1), r].rearrange("b c k w -> (b c) k w"),
                                 xs[r * C:(r + 1) * C, bass.ds(j * N, N)].rearrange("c (k w) -> c k w", w=W)
                                 ).then_inc(out_stored, 16)

            def round_(i, conv, mlp, more):
                if conv:
                    if more:
                        sp.wait_ge(x_loaded, LOAD * i + LOAD)
                        load(i + 1)
                    halos1(i)
                    if more:
                        halos0(i + 1)
                if mlp:
                    store(i - 1)

            sp.wait_ge(zeroed, 3)
            halos0(0)
            round_(0, True, False, True)
            with sp.Fori(1, B - 1) as i:
                round_(i, True, True, True)
            round_(B - 1, True, True, False)
            round_(B, False, True, False)
            sp.wait_ge(out_stored, B * LOAD)

        @block.gpsimd
        def _(pool):
            pool.memset(wnat[:, :, :], 0.0).then_inc(zeroed, 1)
            pool.memset(w5T[:, :], 0.0).then_inc(zeroed, 1)
            pool.memset(halo1[:, :, :], 0.0).then_inc(zeroed, 1)
            for t in (y1, y3):
                pool.memset(t[:, :, 0:1], 0.0).then_inc(zeroed, 1)
                pool.memset(t[:, :, W + 1:W + 2], 0.0).then_inc(zeroed, 1)
            pool.memset(y2[:, :], 0.0).then_inc(zeroed, 1)
            for t in (rowbox, rownear):
                pool.memset(t[:, 0, :], 0.0).then_inc(zeroed, 1)
                pool.memset(t[:, K + 1, :], 0.0).then_inc(zeroed, 1)
            pool.wait_ge(zeroed, 12)
            pool.wait_ge(s_const, 16)

            def scales(i, k):
                n = (i * 4 + k)
                pool.wait_ge(stat_step, n * STAT + STAT)
                pool.tensor_tensor(st[:, 0:1], nv[:, 1:2], const("neg_half"), ALU.pow).then_inc(norm_step, 1)
                pool.wait_ge(norm_step, n * NORM + 1)
                pool.tensor_tensor(st[:, 1:2], gs[:, 2:3], st[:, 0:1], ALU.mult).then_inc(norm_step, 1)
                pool.wait_ge(norm_step, n * NORM + 2)

            def round_(i, more):
                scales(i, 1)
                scales(i, 2)
                scales(i, 3)
                if more:
                    scales(i + 1, 0)

            scales(0, 0)
            with pool.Fori(0, B - 1) as i:
                round_(i, True)
            round_(B - 1, False)

        @block.scalar
        def _(act):
            def normal0(i):
                act.wait_ge(norm_step, i * 4 * NORM + NORM)
                act.activation(y0[:, :, 1:W + 1], sample(i).rearrange("p (k w) -> p k w", w=W), ACT.Identity,
                               bias=st[:, 1:2], scale=st[:, 0:1]).then_inc(y0_written, 1)
                act.wait_ge(y0_written, 3 * i + 1)
                act.copy(y0[:, :, 0:1], y0[:, :, 2:3]).then_inc(y0_written, 1)
                act.copy(y0[:, :, W + 1:W + 2], y0[:, :, W - 1:W]).then_inc(y0_written, 1)

            def normal1(i):
                act.wait_ge(norm_step, i * 4 * NORM + 2 * NORM)
                act.activation(y1[:, :, 1:W + 1], sample(i).rearrange("p (k w) -> p k w", w=W), ACT.Abs,
                               bias=st[:, 1:2], scale=st[:, 0:1]).then_inc(y1_written, 1)

            def softmax_exp(i):
                act.wait_ge(route_step, i * ROUTE + 4)
                act.activation(ex[:, 0:EXPERTS], logit[:, :], ACT.Exp, bias=nmax[:, 0:1],
                               accum_out=ex[:, EXPERTS:EXPERTS + 1]).then_inc(route_exp, 1)

            def elu(j, q, l):
                for a in range(2):
                    act.wait_ge(z_mm, zn(j, q, l, a))
                    act.activation(u[:, a, :], pz[:, a, :], ACT.Relu, scale=-1.0,
                                   bias=s_row[:, l - 1:l] if l else 0.0).then_inc(relu_done, 1)
                    act.wait_ge(relu_done, zn(j, q, l, a))
                    act.activation(u[:, a, :], u[:, a, :], ACT.Exp, scale=-1.0).then_inc(exp_done, 1)

            def phase(i, k, conv, mlp, more):
                j = i - 1
                if mlp:
                    elu(j, k, 0)
                    elu(j, k, 1)
                if k == 3 and more:
                    normal0(i + 1)
                if mlp:
                    elu(j, k, 2)
                if k == 3 and more:
                    softmax_exp(i + 1)
                if k == 0 and conv:
                    normal1(i)
                if mlp:
                    elu(j, k, 3)

            act.wait_ge(s_const, 16)
            act.wait_ge(setup_dve, SETUP_DVE)
            normal0(0)
            softmax_exp(0)
            for k in range(4):
                phase(0, k, True, False, True)
            with act.Fori(1, B - 1) as i:
                for k in range(4):
                    phase(i, k, True, True, True)
            for k in range(4):
                phase(B - 1, k, True, True, False)
            for k in range(4):
                phase(B, k, False, True, False)

        @block.tensor
        def _(pe):
            pe.wait_ge(s_const, 16)
            pe.wait_ge(setup_dve, 1)
            for n in range(M + 3):
                last = pe.transpose(pz.rearrange("p a n -> p (a n)")[:, n * P:(n + 1) * P], wnat[:, n, :], const("ident"))
            last.then_inc(setup_pe, 1)
            pe.matmul(psm[:, 16:16 + C], w5raw[:, :, :].rearrange("k p c -> k (p c)"), const("fold", HID),
                      start=True, stop=True).then_inc(setup_pe, 1)
            pe.wait_ge(setup_dve, 4)
            for l in range(3):
                pe.matmul(psm[:, 64 + l:65 + l], wT[:, M + l, :], const("ones")[:, 0:1], start=True, stop=True)
            for m in range(M):
                last = pe.matmul(psm[32 * m:32 * m + 32, 67:68], w5T[:, :], const("ones")[:, 0:1], start=True, stop=True)
            last.then_inc(setup_pe, 1)

            def group_sums(i, k):
                n = i * 4 + k
                pe.wait_ge(stat_step, n * STAT + Q + 2)
                pe.matmul(psm[:, 0:2], const("group"), ms[:, :], start=True, stop=True)
                last = pe.matmul(psm[:, 2:3], const("neg_group"), ms[:, 0:1], start=True, stop=True)
                if k == 0:
                    last = pe.matmul(psm[:, 3:4], const("chan"), ms[:, 0:1], start=True, stop=True)
                last.then_inc(sums_mm, 1)

            def logits(i):
                pe.wait_ge(route_step, i * ROUTE + 2)
                pe.matmul(psm[:, 8:8 + EXPERTS], const("ones", C), fcp[:, :], start=True, stop=True).then_inc(logits_mm, 1)

            def conv_chunk(i, k, j):
                o = pc[:, j % 2, :]
                n = i * 16 + k * 4 + j
                if not (isinstance(n, int) and n < 2):
                    pe.wait_ge(conv_evac, n - 1)
                if k == 0:
                    if j == 0:
                        pe.wait_ge(y0_written, 3 * i + 3)
                        pe.wait_ge(mix_step, MIX * i + MIX)
                    for kw in range(3):
                        pe.matmul(o, t0[:, kw, :], blocks(y0, j)[:, :, kw:kw + W], start=kw == 0, stop=False)
                    if j == 0:
                        pe.wait_ge(halo0_in, HALO0 * i + HALO0)
                    last = pe.matmul(o, th0[:, :], blocks(halo0, j), start=False, stop=True)
                elif k == 1:
                    if j == 0:
                        pe.wait_ge(y1_written, i + 1)
                    for kw in range(3):
                        pe.matmul(o, t1[:, kw, :], blocks(y1, j)[:, :, kw:kw + W], start=kw == 0, stop=False)
                    if j == 0:
                        pe.wait_ge(halo1_in, HALO1 * i + HALO1)
                    last = pe.matmul(o, th1[:, :], blocks(halo1, j), start=False, stop=True)
                elif k == 2:
                    pe.wait_ge(box_rows, Q * i + min(j + 2, Q))
                    for d, name in enumerate(("box_above", "box_own", "box_below")):
                        last = pe.matmul(o, const(name), rowbox[:, j * KB + d:(j + 1) * KB + d, RAD:RAD + W],
                                         start=d == 0, stop=d == 2)
                else:
                    if j == 0:
                        pe.wait_ge(near_rows, 2 * i + 2)
                    pe.matmul(o, const("near_own"), rownear[:, j * KB + 1:(j + 1) * KB + 1, :], start=True, stop=True)
                    pe.matmul(o[0:32], const("near_above"), rownear[:, j * KB:(j + 1) * KB, :], start=False, stop=True,
                              skip_group_check=True)
                    last = pe.matmul(o[P - 32:P], const("near_below"), rownear[:, j * KB + 2:(j + 1) * KB + 2, :],
                                     start=False, stop=True, skip_group_check=True)
                last.then_inc(conv_mm, 1)

            def layer(j, q, l):
                for a in range(2):
                    n = zn(j, q, l, a)
                    if l == 0:
                        pe.wait_ge(conv_evac, 16 * j + 12 + q + 1)
                    else:
                        pe.wait_ge(g_written, n - 2)
                    for h in range(2):
                        lhsT = wT[:, 2 * a + h, :] if l == 0 else wT[:, M + l - 1, :]
                        rhs = near[:, q * CH:(q + 1) * CH] if l == 0 else g[:, a, h * CH:(h + 1) * CH]
                        last = pe.matmul(pz[:, a, h * CH:(h + 1) * CH], lhsT, rhs, start=True, stop=True)
                    last.then_inc(z_mm, 1)

            def last_layer(j, q):
                pe.wait_ge(g_written, zn(j, q, LAYERS - 1, 1))
                for m in range(M):
                    last = pe.matmul(po[32 * m:32 * m + 32, :], w5T[:, :], g[:, m // 2, (m % 2) * CH:(m % 2 + 1) * CH],
                                     start=True, stop=True)
                last.then_inc(out_mm, 1)

            def phase(i, k, conv, mlp, more):
                j = i - 1
                if mlp:
                    layer(j, k, 0)
                if conv:
                    conv_chunk(i, k, 0)
                    conv_chunk(i, k, 1)
                if k == 3 and more:
                    group_sums(i + 1, 0)
                if mlp:
                    layer(j, k, 1)
                if conv:
                    conv_chunk(i, k, 2)
                    conv_chunk(i, k, 3)
                if k == 3 and more:
                    logits(i + 1)
                if mlp:
                    layer(j, k, 2)
                if conv and k < 3:
                    group_sums(i, k + 1)
                if mlp:
                    layer(j, k, 3)
                    last_layer(j, k)

            group_sums(0, 0)
            logits(0)
            pe.wait_ge(setup_dve, SETUP_DVE)
            for k in range(4):
                phase(0, k, True, False, True)
            with pe.Fori(1, B - 1) as i:
                for k in range(4):
                    phase(i, k, True, True, True)
            for k in range(4):
                phase(B - 1, k, True, True, False)
            for k in range(4):
                phase(B, k, False, True, False)

        @block.vector
        def _(dve):
            dve.wait_ge(s_weights, 16 * N_WEIGHT_DMA)
            dve.wait_ge(s_const, 16)
            dve.wait_ge(zeroed, 2)
            dve.tensor_reduce(w1eff[:, :], w1raw[:, :].rearrange("p (c e) -> p c e", e=8), AX.X, ALU.add).then_inc(folded, 1)
            dve.wait_ge(folded, 1)
            for m in range(M):
                for p in range(2):
                    r = 2 * m + p
                    last = dve.tensor_copy(wnat[p * HID:(p + 1) * HID, m, r * C:(r + 1) * C], w1eff[p * HID:(p + 1) * HID, :])
            last.then_inc(setup_dve, 1)
            dve.wait_ge(setup_pe, 1)
            dve.tensor_copy(wT[:, :, :], pz.rearrange("p a n -> p (a n)")[:, 0:(M + 3) * P].rearrange("p (m n) -> p m n", n=P)
                            ).then_inc(setup_dve, 1)
            dve.wait_ge(setup_pe, 2)
            for p in range(2):
                dve.tensor_scalar(w5T[p * HID:(p + 1) * HID, p * C:(p + 1) * C], psm[p * HID:(p + 1) * HID, 16:16 + C],
                                  0.025, None, ALU.mult).then_inc(setup_dve, 1)
            dve.wait_ge(setup_pe, 3)
            dve.tensor_copy(s_row[:, :], psm[:, 64:68]).then_inc(setup_dve, 1)
            dve.wait_ge(setup_dve, 5)
            dve.tensor_scalar(k_row[:, 0:3], s_row[:, 0:3], -1.0, 1.0, ALU.mult, ALU.add).then_inc(setup_dve, 1)
            dve.tensor_scalar(k_row[:, 3:4], s_row[:, 3:4], -1.0, None, ALU.mult).then_inc(setup_dve, 1)
            for kh in range(3):
                for kw in range(3):
                    if kh:
                        dve.wait_ge(setup_dve, 7 + 3 * kh)
                        dve.scalar_tensor_tensor(out=t1[:, kw, :], in0=const(f"tap{kh}"), scalar=wd[:, 3 * kh + kw:3 * kh + kw + 1],
                                                 in1=t1[:, kw, :], op0=ALU.mult, op1=ALU.add).then_inc(setup_dve, 1)
                    else:
                        dve.tensor_scalar(t1[:, kw, :], const("tap0"), wd[:, kw:kw + 1], None, ALU.mult).then_inc(setup_dve, 1)
            dve.tensor_scalar(th1[:, :], const("halo_tap", HALO), wdh[:, 0:1], None, ALU.mult).then_inc(setup_dve, 1)

            def chunk_stats(i, k, c):
                if k == 0:
                    if c == 0:
                        dve.wait_ge(x_loaded, LOAD * i + LOAD)
                else:
                    dve.wait_ge(conv_evac, i * 16 + (k - 1) * 4 + c + 1)
                dve.nop(nofuse=True)
                dve.bn_stats(bn[:, c, :], sample(i, c)).then_inc(stat_step, 1)

            def merge_stats(i, k):
                n = (i * 4 + k) * STAT
                dve.wait_ge(stat_step, n + Q)
                dve.nop(nofuse=True)
                dve.bn_aggr(ms[:, :], bn[:, :, :].rearrange("p q s -> p (q s)")).then_inc(stat_step, 1)
                dve.wait_ge(stat_step, n + Q + 1)
                dve.scalar_tensor_tensor(out=ms[:, 1:2], in0=ms[:, 0:1], scalar=ms[:, 0:1], in1=ms[:, 1:2],
                                         op0=ALU.mult, op1=ALU.add).then_inc(stat_step, 1)

            def group_var(i, k):
                n = (i * 4 + k) * STAT
                dve.wait_ge(sums_mm, i * 4 + k + 1)
                dve.tensor_copy(gs[:, 0:4 if k == 0 else 3], psm[:, 0:4 if k == 0 else 3]).then_inc(stat_step, 1)
                dve.wait_ge(stat_step, n + Q + 3)
                dve.scalar_tensor_tensor(out=nv[:, 0:1], in0=gs[:, 0:1], scalar=gs[:, 0:1], in1=gs[:, 1:2],
                                         op0=ALU.mult, op1=ALU.subtract).then_inc(stat_step, 1)
                dve.wait_ge(stat_step, n + Q + 4)
                dve.tensor_scalar(nv[:, 1:2], nv[:, 0:1], -1.0, EPS, ALU.mult, ALU.add).then_inc(stat_step, 1)

            def pool_features(i):
                dve.wait_ge(norm_step, i * 4 * NORM + NORM)
                dve.tensor_scalar(pooled[:, :], gs[0:C, 3:4], st[0:C, 0:1], st[0:C, 1:2], ALU.mult, ALU.add).then_inc(route_step, 1)
                dve.wait_ge(route_step, i * ROUTE + 1)
                dve.tensor_scalar(fcp[:, :], fcT[:, :], pooled[:, 0:1], None, ALU.mult).then_inc(route_step, 1)

            def softmax_in(i):
                dve.wait_ge(logits_mm, i + 1)
                dve.tensor_tensor(logit[:, :], psm[:, 8:8 + EXPERTS], fcb[:, :], ALU.add).then_inc(route_step, 1)
                dve.wait_ge(route_step, i * ROUTE + 3)
                dve.tensor_reduce(nmax[:, :], logit[:, :], AX.X, ALU.max, negate=True).then_inc(route_step, 1)

            def mix(i):
                n = MIX * i
                dve.wait_ge(route_exp, i + 1)
                dve.reciprocal(nmax[:, :], ex[:, EXPERTS:EXPERTS + 1]).then_inc(route_step, 1)
                dve.wait_ge(route_step, i * ROUTE + 5)
                dve.tensor_scalar(route[:, :], ex[:, 0:EXPERTS], nmax[:, 0:1], None, ALU.mult).then_inc(mix_step, 1)
                dve.wait_ge(mix_step, n + 1)
                src = [wc[:, e, :, :].rearrange("p o t -> p (o t)") for e in range(EXPERTS)]
                srch = [wh[:, e, :] for e in range(EXPERTS)]
                dve.tensor_scalar(wmix[:, 0, :], src[0], route[:, 0:1], None, ALU.mult).then_inc(mix_step, 1)
                dve.tensor_scalar(whmix[:, 0, :], srch[0], route[0:HALO, 0:1], None, ALU.mult).then_inc(mix_step, 1)
                for e in range(1, EXPERTS):
                    dve.wait_ge(mix_step, n + 1 + 2 * e)
                    dve.scalar_tensor_tensor(out=wmix[:, e % 2, :], in0=src[e], scalar=route[:, e:e + 1],
                                             in1=wmix[:, (e + 1) % 2, :], op0=ALU.mult, op1=ALU.add).then_inc(mix_step, 1)
                    dve.scalar_tensor_tensor(out=whmix[:, e % 2, :], in0=srch[e], scalar=route[0:HALO, e:e + 1],
                                             in1=whmix[:, (e + 1) % 2, :], op0=ALU.mult, op1=ALU.add).then_inc(mix_step, 1)
                dve.wait_ge(mix_step, n + 7)
                mixed = wmix[:, 0, :].rearrange("p (o a b) -> p a b o", a=3, b=3)
                mask = const("tap_mask").rearrange("p (a r) -> p a r", a=3)
                for kh in range(3):
                    for kw in range(3):
                        ins = dve.tensor_tensor(
                            tpart[:, kh, kw, :].rearrange("p (r o) -> p r o", o=C),
                            mixed[:, kh, kw, :].unsqueeze(1).to_broadcast([P, R, C]),
                            mask[:, kh, :].unsqueeze(2).to_broadcast([P, R, C]), ALU.mult)
                    ins.then_inc(mix_step, 1)
                dve.tensor_tensor(th0[:, :].rearrange("p (r o) -> p r o", o=C),
                                  whmix[:, 0, :].unsqueeze(1).to_broadcast([HALO, R, C]),
                                  const("halo_mask", HALO).unsqueeze(2).to_broadcast([HALO, R, C]), ALU.mult).then_inc(mix_step, 1)
                dve.wait_ge(mix_step, n + 10)
                dve.tensor_tensor(t0[:, :, :], tpart[:, 0, :, :], tpart[:, 1, :, :], ALU.add).then_inc(mix_step, 1)
                dve.wait_ge(mix_step, n + 12)
                dve.tensor_tensor(t0[:, :, :], t0[:, :, :], tpart[:, 2, :, :], ALU.add).then_inc(mix_step, 1)

            def evacuate(i, k, c):
                dve.wait_ge(conv_mm, i * 16 + k * 4 + c + 1)
                o = pc[:, c % 2, :]
                if k == 0:
                    ins = dve.scalar_tensor_tensor(out=sample(i, c), in0=o, scalar=bias0[:, 0:1], in1=sample(i, c),
                                                   op0=ALU.add, op1=ALU.add)
                elif k == 1:
                    ins = dve.tensor_tensor(sample(i, c), o, sample(i, c), ALU.add)
                elif k == 2:
                    ins = dve.scalar_tensor_tensor(out=sample(i, c), in0=o, scalar=1.0 / (BOX * BOX), in1=sample(i, c),
                                                   op0=ALU.mult, op1=ALU.add)
                else:
                    ins = dve.tensor_tensor(near[:, c * CH:(c + 1) * CH].rearrange("p (k w) -> p k w", w=W),
                                            o.rearrange("p (k w) -> p k w", w=W), blocks(y3, c)[:, :, 1:W + 1], ALU.subtract)
                ins.then_inc(conv_evac, 1)

            def elu(j, q, l):
                for a in range(2):
                    n = zn(j, q, l, a)
                    dve.wait_ge(exp_done, n)
                    dve.scalar_tensor_tensor(out=g[:, a, :], in0=pz[:, a, :], scalar=k_row[:, l - 1:l] if l else 1.0,
                                             in1=u[:, a, :], op0=ALU.add, op1=ALU.max).then_inc(g_written, 1)

            def output(j, q):
                dve.wait_ge(out_mm, Q * j + q + 1)
                dve.scalar_tensor_tensor(out=sample(j, q), in0=po[:, :], scalar=k_row[:, 3:4], in1=sample(j, q),
                                         op0=ALU.add, op1=ALU.add).then_inc(out_evac, 1)

            def box_scan(i):
                dve.wait_ge(norm_step, i * 4 * NORM + 3 * NORM)
                rows = y2[:, BOX:BOX + K * PITCH].rearrange("p (k w) -> p k w", w=PITCH)[:, :, 0:W]
                dve.tensor_scalar(rows, sample(i).rearrange("p (k w) -> p k w", w=W), st[:, 0:1], st[:, 1:2],
                                  ALU.mult, ALU.add).then_inc(y2_written, 1)
                dve.wait_ge(y2_written, i + 1)
                rb = rowbox[:, 1:K + 1, :].rearrange("p k w -> p (k w)")
                n = KB * PITCH
                for c in range(Q):
                    dve.tensor_tensor_scan(rb[:, c * n:(c + 1) * n], y2[:, c * n + BOX:(c + 1) * n + BOX],
                                           y2[:, c * n:(c + 1) * n], 0.0, ALU.add, ALU.subtract).then_inc(box_rows, 1)

            def near_scan(i):
                dve.wait_ge(norm_step, i * 4 * NORM + 4 * NORM)
                dve.tensor_scalar(y3[:, :, 1:W + 1], sample(i).rearrange("p (k w) -> p k w", w=W), st[:, 0:1],
                                  st[:, 1:2], ALU.mult, ALU.add).then_inc(y3_written, 1)
                dve.wait_ge(y3_written, i + 1)
                dve.tensor_tensor(pairsum[:, :, :], y3[:, :, 0:W], y3[:, :, 1:W + 1], ALU.add).then_inc(near_rows, 1)
                dve.wait_ge(near_rows, 2 * i + 1)
                dve.tensor_tensor(rownear[:, 1:K + 1, :], pairsum[:, :, :], y3[:, :, 2:W + 2], ALU.add).then_inc(near_rows, 1)

            def phase(i, k, conv, mlp, more):
                j = i - 1
                ahead = k == 3 and more
                if ahead:
                    for c in range(Q):
                        chunk_stats(i + 1, 0, c)
                    merge_stats(i + 1, 0)
                if mlp:
                    elu(j, k, 0)
                for c in range(4):
                    if c == 2:
                        if ahead:
                            group_var(i + 1, 0)
                        if mlp:
                            elu(j, k, 1)
                        if ahead:
                            pool_features(i + 1)
                    if conv:
                        evacuate(i, k, c)
                        if k < 3:
                            chunk_stats(i, k + 1, c)
                if conv and k < 3:
                    merge_stats(i, k + 1)
                    if not mlp:
                        group_var(i, k + 1)
                if ahead:
                    softmax_in(i + 1)
                if mlp:
                    elu(j, k, 2)
                    if conv and k < 3:
                        group_var(i, k + 1)
                if ahead:
                    mix(i + 1)
                if mlp:
                    elu(j, k, 3)
                if conv and k == 1:
                    box_scan(i)
                if conv and k == 2:
                    near_scan(i)
                if mlp:
                    output(j, k)

            for c in range(Q):
                chunk_stats(0, 0, c)
            merge_stats(0, 0)
            group_var(0, 0)
            pool_features(0)
            softmax_in(0)
            mix(0)
            for k in range(4):
                phase(0, k, True, False, True)
            with dve.Fori(1, B - 1) as i:
                for k in range(4):
                    phase(i, k, True, True, True)
            for k in range(4):
                phase(B - 1, k, True, True, False)
            for k in range(4):
                phase(B, k, False, True, False)


SETUP_DVE = 7 + 9 + 1
N_WEIGHT_DMA = 8 + 8 + 12 + 1 + 8 + 1 + 4 + 6

_INS = ["x", "L0_conv_w_experts", "L0_conv_bias", "L0_conv_fc_w", "L0_conv_fc_b", "L1_conv_weight",
        "L3_conv_w1", "L3_conv_w2", "L3_conv_w3", "L3_conv_w4", "L3_conv_w5"]


def kernel(**inputs):
    import concourse.bacc as _bacc
    from concourse.bass_utils import run_bass_kernel_spmd as _run

    nc = _bacc.Bacc("TRN2", target_bir_lowering=False, num_devices=1)
    arrays, args = {}, []
    given = {name: np.ascontiguousarray(inputs[name]) for name in _INS}
    given["consts"] = _constants()
    for name, a in given.items():
        arrays[f"in_{name}_dram"] = a
        args.append(nc.dram_tensor(f"in_{name}_dram", a.shape, mybir.dt.from_np(a.dtype), kind="ExternalInput").ap())
    args.append(nc.dram_tensor("out_0_dram", (B, C, H, W), F32, kind="ExternalOutput").ap())
    build(nc, *args)
    r = _run(nc, [arrays], core_ids=[0])
    return r.results[0]["out_0_dram"]
```

```python
from contextlib import ExitStack

import numpy as np

import concourse.bass as bass
from concourse import mybir

F32 = mybir.dt.float32
ALU = mybir.AluOpType
ACT = mybir.ActivationFunctionType
AX = mybir.AxisListType

B, C, H, W = 8, 16, 128, 128
R = 8
K = H // R
P = R * C
N = K * W
Q = 4
KB = K // Q
CH = KB * W
EXPERTS = 3
HID = 64
M = P // 32
BOX = 17
RAD = BOX // 2
PITCH = W + BOX
EPS = 1e-5
HALO = 6 * C
LAYERS = 4

CONSTS = {}


def _constants():
    r, c = np.divmod(np.arange(P), C)
    dr = r[None, :] - r[:, None]
    same = c[None, :] == c[:, None]
    parts = [("ident", np.eye(P)),
             ("group", (c[None, :] // 2 == c[:, None] // 2) / (2 * R)),
             ("neg_group", (c[None, :] // 2 == c[:, None] // 2) / (-2.0 * R)),
             ("chan", same / R)]
    for kh in range(3):
        parts.append((f"tap{kh}", same & (dr == 1 - kh)))
    parts += [("box_above", same & (dr <= 0)), ("box_own", same), ("box_below", same & (dr >= 0))]
    parts += [("near_own", same & (abs(dr) <= 1)),
              ("near_above", (same & (dr == 1 - R))[:, 0:32]),
              ("near_below", (same & (dr == R - 1))[:, P - 32:P])]
    hk = np.arange(P) % (2 * C)
    below, hc = np.divmod(hk, C)
    edge = np.where(below, R - 1, 0)[:, None]
    parts.append(("halo_tap", (hc[:, None] == c[None, :]) & (edge == r[None, :])))
    parts.append(("tap_mask", np.stack([np.arange(R)[None, :] == r[:, None] - kh + 1 for kh in range(3)], 1)))
    parts.append(("halo_mask", edge == np.arange(R)[None, :]))
    o = np.arange(P) % HID
    parts.append(("fold", (o // 32 * 8 + o % 8)[:, None] == np.arange(C)[None, :]))
    parts.append(("ones", np.ones((P, P))))
    parts.append(("neg_half", np.full((P, 1), -0.5)))
    parts.append(("spread", np.arange(P)[:, None] == c[None, :]))
    for n in range(6):
        h = np.arange(HALO)[None, :]
        parts.append((f"spread_halo{n}", (h // C == n) & (h % C == np.arange(P)[:, None])))
    at, cols = 0, []
    for name, m in parts:
        m = np.asarray(m, np.float32).reshape(P, -1)
        CONSTS[name] = (at, m.shape[1])
        cols.append(m)
        at += m.shape[1]
    return np.concatenate(cols, axis=1)


def build(nc, x, w_experts, conv_bias, fc_w, fc_b, w_depth, w1, w2, w3, w4, w5, consts, out):
    NCON = consts.shape[1]
    with ExitStack() as ctx:
        def sb(name, shape):
            return ctx.enter_context(nc.sbuf_tensor(name, shape, F32))

        def pb(name, shape):
            return ctx.enter_context(nc.psum_tensor(name, shape, F32))

        def sem(name):
            return ctx.enter_context(nc.semaphore(name))

        con = sb("con", [P, NCON])

        def const(name, rows=P):
            at, n = CONSTS[name]
            return con[0:rows, at:at + n]

        xs = sb("xs", [P, B * N])
        y0 = sb("y0", [P, K, W + 2])
        y1 = sb("y1", [P, K, W + 2])
        y2 = sb("y2", [P, K * PITCH + BOX])
        y3 = sb("y3", [P, K, W + 2])
        halo0 = sb("halo0", [HALO, K, W])
        halo1 = sb("halo1", [HALO, K, W])
        rowbox = sb("rowbox", [P, K + 2, PITCH])
        pairsum = sb("pairsum", [P, K, W])
        rownear = sb("rownear", [P, K + 2, W])
        near = sb("near", [P, N])
        u = sb("u", [P, M, CH])
        g = sb("g", [P, M, CH])

        wc_in = sb("wc_in", [C, EXPERTS * C, 9])
        wd_in = sb("wd_in", [C, 9])
        bias_in = sb("bias_in", [C, 1])
        fcb_in = sb("fcb_in", [1, EXPERTS])
        wc = sb("wc", [P, EXPERTS, C, 9])
        wh = sb("wh", [HALO, EXPERTS, C])
        wmix = sb("wmix", [P, 2, C * 9])
        whmix = sb("whmix", [HALO, 2, C])
        t0 = sb("t0", [P, 3, P])
        tpart = sb("tpart", [P, 3, 3, P])
        th0 = sb("th0", [HALO, P])
        wd = sb("wd", [P, 9])
        wdh = sb("wdh", [HALO, 1])
        t1 = sb("t1", [P, 3, P])
        th1 = sb("th1", [HALO, P])
        bias0 = sb("bias0", [P, 1])
        fcT = sb("fcT", [C, EXPERTS])
        fcb = sb("fcb", [P, EXPERTS])

        w1raw = sb("w1raw", [P, P])
        w1eff = sb("w1eff", [P, C])
        wnat = sb("wnat", [P, M + 3, P])
        wT = sb("wT", [P, M + 3, P])
        w5raw = sb("w5raw", [HID, 2, HID])
        w5T = sb("w5T", [P, 32])
        s_row = sb("s_row", [P, 4])
        k_row = sb("k_row", [P, 3])
        n_row = sb("n_row", [P, 4])

        bn = [sb(f"bn{k}", [P, Q, 6]) for k in range(4)]
        ms = [sb(f"ms{k}", [P, 2]) for k in range(4)]
        gs = [sb(f"gs{k}", [P, 4]) for k in range(4)]
        nv = [sb(f"nv{k}", [P, 2]) for k in range(4)]
        st = [sb(f"st{k}", [P, 2]) for k in range(4)]
        pooled = sb("pooled", [C, 1])
        fcp = sb("fcp", [C, EXPERTS])
        logit = sb("logit", [P, EXPERTS])
        nmax = sb("nmax", [P, 1])
        ex = sb("ex", [P, EXPERTS + 1])
        route = sb("route", [P, EXPERTS])

        pz = pb("pz", [P, M, CH])
        pc = pb("pc", [P, 2, CH])
        po = pb("po", [P, CH])
        psm = pb("psm", [P, 512])

        s_const = sem("s_const")
        s_weights = sem("s_weights")
        x_loaded = sem("x_loaded")
        zeroed = sem("zeroed")
        setup_dve = sem("setup_dve")
        setup_pe = sem("setup_pe")
        setup_pool = sem("setup_pool")
        stat_step = [sem(f"stat_step{k}") for k in range(4)]
        sums_mm = [sem(f"sums_mm{k}") for k in range(4)]
        norm_step = [sem(f"norm_step{k}") for k in range(4)]
        y0_written = sem("y0_written")
        y1_written = sem("y1_written")
        y2_written = sem("y2_written")
        y3_written = sem("y3_written")
        box_rows = sem("box_rows")
        near_rows = sem("near_rows")
        halo0_in = sem("halo0_in")
        halo1_in = sem("halo1_in")
        conv_mm = [sem(f"conv_mm{k}") for k in range(4)]
        conv_evac = [sem(f"conv_evac{k}") for k in range(4)]
        route_step = sem("route_step")
        logits_mm = sem("logits_mm")
        route_exp = sem("route_exp")
        mix_step = sem("mix_step")
        spread_step = sem("spread_step")
        folded = sem("folded")
        z_mm = sem("z_mm")
        relu_done = sem("relu_done")
        clip_done = sem("clip_done")
        exp_done = sem("exp_done")
        g_written = sem("g_written")
        out_mm = sem("out_mm")
        out_evac = sem("out_evac")
        out_stored = sem("out_stored")

        xv = x.rearrange("b c (k r) w -> b r c k w", r=R)
        ov = out.rearrange("b c (k r) w -> b r c k w", r=R)

        def sample(i, j=None):
            if j is None:
                return xs[:, bass.ds(i * N, N)]
            return xs[:, bass.ds(i * N + j * CH, CH)]

        def blocks(t, j):
            return t[:, j * KB:(j + 1) * KB, :]

        STAT = Q + 5
        NORM = 2
        ROUTE = 6
        MIX = 6
        SPREAD = 6
        HALO0 = 12 * 16
        HALO1 = 6 * 16
        LOAD = R * 16

        def zn(j, q, l, m):
            return j * (Q * LAYERS * M) + (q * LAYERS + l) * M + m + 1

        CLIP = ()
        CLIP_LAST = (0, 2)

        def clips(j):
            return CLIP_LAST if isinstance(j, int) and j == B - 1 else CLIP

        def clip_n(j, q, l, m):
            c = clips(j)
            return j * (Q * LAYERS * len(CLIP)) + (q * LAYERS + l) * len(c) + c.index(m) + 1

        def relu_n(j, q, l, m):
            c = [a for a in range(M) if a not in clips(j)]
            return j * (Q * LAYERS * (M - len(CLIP))) + (q * LAYERS + l) * len(c) + c.index(m) + 1

        LAYER = (0, 2, 1, 3)
        AHEAD = (1, 0, 1, 0)

        NEXT = {0: 1, 1: 2, 2: 3}

        def work(t, p, early, late):
            k, i = LAYER[p], t + AHEAD[p]
            return (k, i) if (early if AHEAD[p] else late) else None

        def before(t, p, early, late):
            if p == 0:
                return None if isinstance(t, int) and t < 0 else (1, 0) if isinstance(t, int) and t == 0 else (3, t - 1)
            for q in range(p - 1, -1, -1):
                if work(t, q, early, late):
                    return work(t, q, early, late)
            return (3, t - 1)

        def rounds(eng, one):
            one(-1, True, False, False, True)
            one(0, True, True, False, True)
            with eng.Fori(1, B - 2) as t:
                one(t, True, True, True, True)
            one(B - 2, True, True, True, False)
            one(B - 1, False, True, True, False)
            one(B, False, False, True, False)

        block = ctx.enter_context(nc.Block())

        @block.sync
        def _(sp):
            def load(i):
                for r in range(R):
                    sp.dma_start(xs[r * C:(r + 1) * C, bass.ds(i * N, N)].rearrange("c (k w) -> c k w", w=W),
                                 xv[i, r]
                                 ).then_inc(x_loaded, 16)

            load(0)
            sp.dma_start(con[:, :], consts).then_inc(s_const, 16)
            def halos0(i):
                sp.wait_ge(y0_written, 3 * i + 3)
                for kw in range(3):
                    a, b = kw * 2 * C, (kw * 2 + 1) * C
                    for dst, rows in ((halo0[a:a + C, 1:K], y0[(R - 1) * C:P, 0:K - 1, kw:kw + W]),
                                      (halo0[a:a + C, 0:1], y0[C:2 * C, 0:1, kw:kw + W]),
                                      (halo0[b:b + C, 0:K - 1], y0[0:C, 1:K, kw:kw + W]),
                                      (halo0[b:b + C, K - 1:K], y0[(R - 2) * C:(R - 1) * C, K - 1:K, kw:kw + W])):
                        sp.dma_start(dst, rows).then_inc(halo0_in, 16)

            def halos1(i):
                sp.wait_ge(y1_written, i + 1)
                for kw in range(3):
                    a, b = kw * 2 * C, (kw * 2 + 1) * C
                    for dst, rows in ((halo1[a:a + C, 1:K], y1[(R - 1) * C:P, 0:K - 1, kw:kw + W]),
                                      (halo1[b:b + C, 0:K - 1], y1[0:C, 1:K, kw:kw + W])):
                        sp.dma_start(dst, rows).then_inc(halo1_in, 16)

            def store(j):
                sp.wait_ge(out_evac, Q * j + Q)
                for r in range(R):
                    sp.dma_start(ov[j, r] if isinstance(j, int) else ov[bass.ds(j, 1), r].rearrange("b c k w -> (b c) k w"),
                                 xs[r * C:(r + 1) * C, bass.ds(j * N, N)].rearrange("c (k w) -> c k w", w=W)
                                 ).then_inc(out_stored, 16)

            def one(t, early, late, mlp, more):
                if early:
                    halos1(t + 1)
                if isinstance(t, int) and t < 1:
                    for i in range(2 + 3 * (t + 1), 5 + 3 * (t + 1)):
                        sp.wait_ge(x_loaded, LOAD * i)
                        load(i)
                if more:
                    halos0(t + 2)
                if mlp:
                    store(t - 1)

            sp.wait_ge(zeroed, 3)
            halos0(0)
            sp.wait_ge(x_loaded, LOAD)
            load(1)
            rounds(sp, one)
            sp.wait_ge(out_stored, B * LOAD)

        @block.gpsimd
        def _(pool):
            pool.memset(wnat[:, :, :], 0.0).then_inc(zeroed, 1)
            pool.memset(w5T[:, :], 0.0).then_inc(zeroed, 1)
            pool.memset(halo1[:, :, :], 0.0).then_inc(zeroed, 1)
            for t in (y1, y3):
                pool.memset(t[:, :, 0:1], 0.0).then_inc(zeroed, 1)
                pool.memset(t[:, :, W + 1:W + 2], 0.0).then_inc(zeroed, 1)
            pool.memset(y2[:, :], 0.0).then_inc(zeroed, 1)
            for t in (rowbox, rownear):
                pool.memset(t[:, 0, :], 0.0).then_inc(zeroed, 1)
                pool.memset(t[:, K + 1, :], 0.0).then_inc(zeroed, 1)
            pool.wait_ge(zeroed, 12)
            pool.wait_ge(s_const, 16)

            def scales(i, k):
                pool.wait_ge(stat_step[k], i * STAT + STAT)
                pool.tensor_tensor(st[k][:, 0:1], nv[k][:, 1:2], const("neg_half"), ALU.pow).then_inc(norm_step[k], 1)
                pool.wait_ge(norm_step[k], i * NORM + 1)
                pool.tensor_tensor(st[k][:, 1:2], gs[k][:, 2:3], st[k][:, 0:1], ALU.mult).then_inc(norm_step[k], 1)

            def spread(i):
                pool.wait_ge(mix_step, i * MIX + MIX)
                mixed = wmix[:, 0, :].rearrange("p (o a b) -> p a b o", a=3, b=3)
                mask = const("tap_mask").rearrange("p (a r) -> p a r", a=3)
                for kh in range(3):
                    for kw in range(3):
                        ins = pool.tensor_tensor(
                            tpart[:, kh, kw, :].rearrange("p (r o) -> p r o", o=C),
                            mixed[:, kh, kw, :].unsqueeze(1).to_broadcast([P, R, C]),
                            mask[:, kh, :].unsqueeze(2).to_broadcast([P, R, C]), ALU.mult)
                    ins.then_inc(spread_step, 1)
                pool.tensor_tensor(th0[:, :].rearrange("p (r o) -> p r o", o=C),
                                   whmix[:, 0, :].unsqueeze(1).to_broadcast([HALO, R, C]),
                                   const("halo_mask", HALO).unsqueeze(2).to_broadcast([HALO, R, C]), ALU.mult).then_inc(spread_step, 1)
                pool.wait_ge(spread_step, i * SPREAD + 3)
                pool.tensor_tensor(t0[:, :, :], tpart[:, 0, :, :], tpart[:, 1, :, :], ALU.add).then_inc(spread_step, 1)
                pool.wait_ge(spread_step, i * SPREAD + 5)
                pool.tensor_tensor(t0[:, :, :], t0[:, :, :], tpart[:, 2, :, :], ALU.add).then_inc(spread_step, 1)

            def one(t, early, late, mlp, more):
                if more:
                    scales(t + 2, 0)
                if early:
                    scales(t + 1, 1)
                if late:
                    scales(t, 3)
                if more:
                    spread(t + 2)
                if early:
                    scales(t + 1, 2)

            scales(0, 0)
            spread(0)
            rounds(pool, one)

        @block.scalar
        def _(act):
            with nc.allow_non_contiguous_dma(reason="small weights, once"):
                act.dma_start(wc_in[:, :, :], w_experts.rearrange("n o c a b -> c (n o) (a b)")).then_inc(s_weights, 16)
                act.dma_start(wd_in[:, :], w_depth.rearrange("c z a b -> c (z a b)")).then_inc(s_weights, 16)
                act.dma_start(bias_in[:, :], conv_bias.rearrange("(c z) -> c z", z=1)).then_inc(s_weights, 16)
                act.dma_start(fcT[:, :], fc_w.rearrange("n c -> c n")).then_inc(s_weights, 16)
            act.dma_start(fcb_in[:, :], fc_b.rearrange("(z n) -> z n", z=1)).then_inc(s_weights, 16)
            for p in range(2):
                act.dma_start(w1raw[p * HID:(p + 1) * HID, :], w1).then_inc(s_weights, 16)
                act.dma_start(w5raw[:, p, :], w5).then_inc(s_weights, 16)
            act.wait_ge(zeroed, 1)
            for p in range(2):
                for l, w in enumerate((w2, w3, w4)):
                    act.dma_start(wnat[p * HID:(p + 1) * HID, M + l, p * HID:(p + 1) * HID], w).then_inc(s_weights, 16)

            def normal0(i):
                act.wait_ge(norm_step[0], i * NORM + NORM)
                act.activation(y0[:, :, 1:W + 1], sample(i).rearrange("p (k w) -> p k w", w=W), ACT.Identity,
                               bias=st[0][:, 1:2], scale=st[0][:, 0:1]).then_inc(y0_written, 1)
                act.wait_ge(y0_written, 3 * i + 1)
                act.copy(y0[:, :, 0:1], y0[:, :, 2:3]).then_inc(y0_written, 1)
                act.copy(y0[:, :, W + 1:W + 2], y0[:, :, W - 1:W]).then_inc(y0_written, 1)

            def normal1(i):
                act.wait_ge(norm_step[1], i * NORM + NORM)
                act.activation(y1[:, :, 1:W + 1], sample(i).rearrange("p (k w) -> p k w", w=W), ACT.Abs,
                               bias=st[1][:, 1:2], scale=st[1][:, 0:1]).then_inc(y1_written, 1)

            def softmax_exp(i):
                act.wait_ge(route_step, i * ROUTE + 4)
                act.activation(ex[:, 0:EXPERTS], logit[:, :], ACT.Exp, bias=nmax[:, 0:1],
                               accum_out=ex[:, EXPERTS:EXPERTS + 1]).then_inc(route_exp, 1)

            def elu(j, q, l):
                def relu(m):
                    act.wait_ge(z_mm, zn(j, q, l, m))
                    act.activation(u[:, m, :], pz[:, m, :], ACT.Relu, scale=-1.0,
                                   bias=s_row[:, l - 1:l] if l else 0.0).then_inc(relu_done, 1)

                def exp(m):
                    if m in clips(j):
                        act.wait_ge(clip_done, clip_n(j, q, l, m))
                        act.activation(u[:, m, :], u[:, m, :], ACT.Exp).then_inc(exp_done, 1)
                    else:
                        act.wait_ge(relu_done, relu_n(j, q, l, m))
                        act.activation(u[:, m, :], u[:, m, :], ACT.Exp, scale=-1.0).then_inc(exp_done, 1)

                if clips(j):
                    relu(1)
                    exp(0)
                    exp(1)
                    exp(2)
                    relu(3)
                    exp(3)
                else:
                    relu(0)
                    for m in range(1, M):
                        relu(m)
                        exp(m - 1)
                    exp(M - 1)

            def one(t, early, late, mlp, more):
                for p in range(4):
                    for l in range(LAYERS):
                        if mlp:
                            elu(t - 1, p, l)
                        if p == 1 and l == 1 and early:
                            normal1(t + 1)
                        if p == 1 and l == 2 and more:
                            softmax_exp(t + 2)
                        if p == 2 and l == 0 and more:
                            normal0(t + 2)

            act.wait_ge(s_const, 16)
            normal0(0)
            softmax_exp(0)
            act.wait_ge(setup_dve, SETUP_DVE)
            rounds(act, one)

        @block.tensor
        def _(pe):
            pe.wait_ge(s_const, 16)
            pe.wait_ge(s_weights, 16 * N_WEIGHT_DMA)

            pe.matmul(pc[:, 0, 0:EXPERTS * C * 9], const("spread", C), wc_in[:, :, :].rearrange("c n t -> c (n t)"),
                      start=True, stop=True)
            pe.matmul(pc[:, 0, 500:509], const("spread", C), wd_in[:, :], start=True, stop=True)
            pe.matmul(pc[:, 0, 510:511], const("spread", C), bias_in[:, :], start=True, stop=True)
            pe.matmul(pc[:, 0, 440:440 + EXPERTS], const("ones", 1), fcb_in[:, :], start=True, stop=True)
            taps = [2 * below * 3 + kw for kw in range(3) for below in range(2)]
            for n, tap in enumerate(taps):
                pe.matmul(pc[0:HALO, 1, 0:EXPERTS * C], const(f"spread_halo{n}", C), wc_in[:, :, tap], start=n == 0, stop=n == 5)
            for n, tap in enumerate(taps):
                last = pe.matmul(pc[0:HALO, 1, 100:101], const(f"spread_halo{n}", C), wd_in[:, tap:tap + 1], start=n == 0, stop=n == 5)
            last.then_inc(setup_pe, 1)
            def group_sums(i, k):
                pe.wait_ge(stat_step[k], i * STAT + Q + 2)
                pe.matmul(psm[:, 0:2], const("group"), ms[k][:, :], start=True, stop=True)
                last = pe.matmul(psm[:, 2:3], const("neg_group"), ms[k][:, 0:1], start=True, stop=True)
                if k == 0:
                    last = pe.matmul(psm[:, 3:4], const("chan"), ms[k][:, 0:1], start=True, stop=True)
                last.then_inc(sums_mm[k], 1)

            def logits(i):
                pe.wait_ge(route_step, i * ROUTE + 2)
                pe.matmul(psm[:, 8:8 + EXPERTS], const("ones", C), fcp[:, :], start=True, stop=True).then_inc(logits_mm, 1)

            def conv_chunk(i, k, j, last_conv):
                o = pc[:, j % 2, :]
                if j >= 2:
                    pe.wait_ge(conv_evac[k], Q * i + j - 1)
                elif last_conv:
                    pe.wait_ge(conv_evac[last_conv[0]], Q * last_conv[1] + j + 3)
                if k == 0:
                    if j == 0:
                        pe.wait_ge(y0_written, 3 * i + 3)
                        pe.wait_ge(spread_step, SPREAD * i + SPREAD)
                    for kw in range(3):
                        pe.matmul(o, t0[:, kw, :], blocks(y0, j)[:, :, kw:kw + W], start=kw == 0, stop=False)
                    if j == 0:
                        pe.wait_ge(halo0_in, HALO0 * i + HALO0)
                    last = pe.matmul(o, th0[:, :], blocks(halo0, j), start=False, stop=True)
                elif k == 1:
                    if j == 0:
                        pe.wait_ge(y1_written, i + 1)
                    for kw in range(3):
                        pe.matmul(o, t1[:, kw, :], blocks(y1, j)[:, :, kw:kw + W], start=kw == 0, stop=False)
                    if j == 0:
                        pe.wait_ge(halo1_in, HALO1 * i + HALO1)
                    last = pe.matmul(o, th1[:, :], blocks(halo1, j), start=False, stop=True)
                elif k == 2:
                    pe.wait_ge(box_rows, Q * i + min(j + 2, Q))
                    for d, name in enumerate(("box_above", "box_own", "box_below")):
                        last = pe.matmul(o, const(name), rowbox[:, j * KB + d:(j + 1) * KB + d, RAD:RAD + W],
                                         start=d == 0, stop=d == 2)
                else:
                    if j == 0:
                        pe.wait_ge(near_rows, 2 * i + 2)
                    pe.matmul(o, const("near_own"), rownear[:, j * KB + 1:(j + 1) * KB + 1, :], start=True, stop=True)
                    pe.matmul(o[0:32], const("near_above"), rownear[:, j * KB:(j + 1) * KB, :], start=False, stop=True,
                              skip_group_check=True)
                    last = pe.matmul(o[P - 32:P], const("near_below"), rownear[:, j * KB + 2:(j + 1) * KB + 2, :],
                                     start=False, stop=True, skip_group_check=True)
                last.then_inc(conv_mm[k], 1)

            def layer(j, q, l):
                for m in range(M):
                    if l == 0:
                        if m == 0:
                            pe.wait_ge(conv_evac[3], Q * j + q + 1)
                        pe.matmul(pz[:, m, :], wT[:, m, :], near[:, q * CH:(q + 1) * CH],
                                  start=True, stop=True).then_inc(z_mm, 1)
                    else:
                        pe.wait_ge(g_written, zn(j, q, l - 1, m))
                        pe.matmul(pz[:, m, :], wT[:, M + l - 1, :], g[:, m, :],
                                  start=True, stop=True).then_inc(z_mm, 1)

            def last_layer(j, q):
                pe.wait_ge(g_written, zn(j, q, LAYERS - 1, M - 1))
                for m in range(M):
                    last = pe.matmul(po[32 * m:32 * m + 32, :], w5T[:, :], g[:, m, :],
                                     start=True, stop=True)
                last.then_inc(out_mm, 1)

            def one(t, early, late, mlp, more):
                for p in range(4):
                    conv = work(t, p, early, late)
                    prev = work(t, p - 1, early, late) if p else None
                    for l in range(LAYERS):
                        if mlp:
                            layer(t - 1, p, l)
                        if l == 0 and prev and prev[0] != 3:
                            group_sums(prev[1], NEXT[prev[0]])
                        if p == 0 and l == 2 and more:
                            group_sums(t + 2, 0)
                        if p == 1 and l == 1 and more:
                            logits(t + 2)
                        if conv:
                            conv_chunk(conv[1], conv[0], l, before(t, p, early, late))
                    if mlp:
                        last_layer(t - 1, p)

            group_sums(0, 0)
            logits(0)
            pe.wait_ge(setup_dve, 3)
            for n in range(M + 3):
                last = pe.transpose(pz[:, :, :].rearrange("p a n -> p (a n)")[:, n * P:(n + 1) * P], wnat[:, n, :], const("ident"))
            last.then_inc(setup_pe, 1)
            pe.matmul(psm[:, 16:16 + C], w5raw[:, :, :].rearrange("k p c -> k (p c)"), const("fold", HID),
                      start=True, stop=True).then_inc(setup_pe, 1)
            pe.wait_ge(setup_dve, 6)
            for l in range(3):
                pe.matmul(psm[:, 64 + l:65 + l], wT[:, M + l, :], const("ones")[:, 0:1], start=True, stop=True)
            for m in range(M):
                last = pe.matmul(psm[32 * m:32 * m + 32, 67:68], w5T[:, :], const("ones")[:, 0:1], start=True, stop=True)
            last.then_inc(setup_pe, 1)
            pe.wait_ge(setup_dve, SETUP_DVE)
            rounds(pe, one)

        @block.vector
        def _(dve):
            def setup_channels():
                dve.wait_ge(setup_pe, 1)
                dve.tensor_copy(wc[:, :, :, :].rearrange("p n o t -> p (n o t)"), pc[:, 0, 0:EXPERTS * C * 9])
                dve.tensor_copy(wd[:, :], pc[:, 0, 500:509])
                dve.tensor_copy(bias0[:, :], pc[:, 0, 510:511])
                dve.tensor_copy(fcb[:, :], pc[:, 0, 440:440 + EXPERTS])
                dve.tensor_copy(wh[:, :, :].rearrange("p n o -> p (n o)"), pc[0:HALO, 1, 0:EXPERTS * C])
                dve.tensor_copy(wdh[:, :], pc[0:HALO, 1, 100:101]).then_inc(setup_dve, 1)

            def setup_perceptron():
                dve.wait_ge(s_weights, 16 * N_WEIGHT_DMA)
                dve.wait_ge(zeroed, 2)
                dve.tensor_reduce(w1eff[:, :], w1raw[:, :].rearrange("p (c e) -> p c e", e=8), AX.X, ALU.add).then_inc(setup_dve, 1)
                dve.wait_ge(setup_dve, 2)
                for m in range(M):
                    for p in range(2):
                        r = 2 * m + p
                        last = dve.tensor_copy(wnat[p * HID:(p + 1) * HID, m, r * C:(r + 1) * C], w1eff[p * HID:(p + 1) * HID, :])
                last.then_inc(setup_dve, 1)
                dve.wait_ge(setup_pe, 2)
                dve.tensor_copy(wT[:, :, :], pz[:, :, :].rearrange("p a n -> p (a n)")[:, 0:(M + 3) * P].rearrange("p (m n) -> p m n", n=P)
                                ).then_inc(setup_dve, 1)
                dve.wait_ge(setup_pe, 3)
                for p in range(2):
                    dve.tensor_scalar(w5T[p * HID:(p + 1) * HID, p * C:(p + 1) * C], psm[p * HID:(p + 1) * HID, 16:16 + C],
                                      0.025, None, ALU.mult).then_inc(setup_dve, 1)
                dve.wait_ge(setup_pe, 4)
                dve.tensor_copy(s_row[:, :], psm[:, 64:68]).then_inc(setup_dve, 1)
                dve.wait_ge(setup_dve, 7)
                dve.tensor_scalar(k_row[:, 0:3], s_row[:, 0:3], -1.0, 1.0, ALU.mult, ALU.add).then_inc(setup_dve, 1)
                dve.tensor_scalar(n_row[:, :], s_row[:, :], -1.0, None, ALU.mult).then_inc(setup_dve, 1)
                for kh in range(3):
                    for kw in range(3):
                        if kh:
                            dve.wait_ge(setup_dve, 9 + 3 * kh)
                            dve.scalar_tensor_tensor(out=t1[:, kw, :], in0=const(f"tap{kh}"), scalar=wd[:, 3 * kh + kw:3 * kh + kw + 1],
                                                     in1=t1[:, kw, :], op0=ALU.mult, op1=ALU.add).then_inc(setup_dve, 1)
                        else:
                            dve.tensor_scalar(t1[:, kw, :], const("tap0"), wd[:, kw:kw + 1], None, ALU.mult).then_inc(setup_dve, 1)
                dve.tensor_scalar(th1[:, :], const("halo_tap", HALO), wdh[:, 0:1], None, ALU.mult).then_inc(setup_dve, 1)

            def chunk_stats(i, k, c):
                if k == 0:
                    if c == 0:
                        dve.wait_ge(x_loaded, LOAD * i + LOAD)
                else:
                    dve.wait_ge(conv_evac[k - 1], Q * i + c + 1)
                dve.nop(nofuse=True)
                dve.bn_stats(bn[k][:, c, :], sample(i, c)).then_inc(stat_step[k], 1)

            def merge_stats(i, k):
                dve.wait_ge(stat_step[k], i * STAT + Q)
                dve.nop(nofuse=True)
                dve.bn_aggr(ms[k][:, :], bn[k][:, :, :].rearrange("p q s -> p (q s)")).then_inc(stat_step[k], 1)
                dve.wait_ge(stat_step[k], i * STAT + Q + 1)
                dve.scalar_tensor_tensor(out=ms[k][:, 1:2], in0=ms[k][:, 0:1], scalar=ms[k][:, 0:1], in1=ms[k][:, 1:2],
                                         op0=ALU.mult, op1=ALU.add).then_inc(stat_step[k], 1)

            def group_var(i, k):
                n = 4 if k == 0 else 3
                dve.wait_ge(sums_mm[k], i + 1)
                dve.tensor_copy(gs[k][:, 0:n], psm[:, 0:n]).then_inc(stat_step[k], 1)
                dve.wait_ge(stat_step[k], i * STAT + Q + 3)
                dve.scalar_tensor_tensor(out=nv[k][:, 0:1], in0=gs[k][:, 0:1], scalar=gs[k][:, 0:1], in1=gs[k][:, 1:2],
                                         op0=ALU.mult, op1=ALU.subtract).then_inc(stat_step[k], 1)
                dve.wait_ge(stat_step[k], i * STAT + Q + 4)
                dve.tensor_scalar(nv[k][:, 1:2], nv[k][:, 0:1], -1.0, EPS, ALU.mult, ALU.add).then_inc(stat_step[k], 1)

            def pool_features(i):
                dve.wait_ge(norm_step[0], i * NORM + NORM)
                dve.tensor_scalar(pooled[:, :], gs[0][0:C, 3:4], st[0][0:C, 0:1], st[0][0:C, 1:2], ALU.mult, ALU.add).then_inc(route_step, 1)
                dve.wait_ge(route_step, i * ROUTE + 1)
                dve.tensor_scalar(fcp[:, :], fcT[:, :], pooled[:, 0:1], None, ALU.mult).then_inc(route_step, 1)

            def softmax_in(i):
                dve.wait_ge(logits_mm, i + 1)
                dve.tensor_tensor(logit[:, :], psm[:, 8:8 + EXPERTS], fcb[:, :], ALU.add).then_inc(route_step, 1)
                dve.wait_ge(route_step, i * ROUTE + 3)
                dve.tensor_reduce(nmax[:, :], logit[:, :], AX.X, ALU.max, negate=True).then_inc(route_step, 1)

            def mix(i):
                n = MIX * i
                dve.wait_ge(route_exp, i + 1)
                dve.reciprocal(nmax[:, :], ex[:, EXPERTS:EXPERTS + 1]).then_inc(route_step, 1)
                dve.wait_ge(route_step, i * ROUTE + 5)
                dve.tensor_scalar(route[:, :], ex[:, 0:EXPERTS], nmax[:, 0:1], None, ALU.mult).then_inc(route_step, 1)
                dve.wait_ge(route_step, i * ROUTE + 6)
                src = [wc[:, e, :, :].rearrange("p o t -> p (o t)") for e in range(EXPERTS)]
                srch = [wh[:, e, :] for e in range(EXPERTS)]
                dve.tensor_scalar(wmix[:, 0, :], src[0], route[:, 0:1], None, ALU.mult).then_inc(mix_step, 1)
                dve.tensor_scalar(whmix[:, 0, :], srch[0], route[0:HALO, 0:1], None, ALU.mult).then_inc(mix_step, 1)
                for e in range(1, EXPERTS):
                    dve.wait_ge(mix_step, n + 2 * e)
                    dve.scalar_tensor_tensor(out=wmix[:, e % 2, :], in0=src[e], scalar=route[:, e:e + 1],
                                             in1=wmix[:, (e + 1) % 2, :], op0=ALU.mult, op1=ALU.add).then_inc(mix_step, 1)
                    dve.scalar_tensor_tensor(out=whmix[:, e % 2, :], in0=srch[e], scalar=route[0:HALO, e:e + 1],
                                             in1=whmix[:, (e + 1) % 2, :], op0=ALU.mult, op1=ALU.add).then_inc(mix_step, 1)

            def evacuate(i, k, c):
                dve.wait_ge(conv_mm[k], Q * i + c + 1)
                o = pc[:, c % 2, :]
                if k == 0:
                    ins = dve.scalar_tensor_tensor(out=sample(i, c), in0=o, scalar=bias0[:, 0:1], in1=sample(i, c),
                                                   op0=ALU.add, op1=ALU.add)
                elif k == 1:
                    ins = dve.tensor_tensor(sample(i, c), o, sample(i, c), ALU.add)
                elif k == 2:
                    ins = dve.scalar_tensor_tensor(out=sample(i, c), in0=o, scalar=1.0 / (BOX * BOX), in1=sample(i, c),
                                                   op0=ALU.mult, op1=ALU.add)
                else:
                    ins = dve.tensor_tensor(near[:, c * CH:(c + 1) * CH].rearrange("p (k w) -> p k w", w=W),
                                            o.rearrange("p (k w) -> p k w", w=W), blocks(y3, c)[:, :, 1:W + 1], ALU.subtract)
                ins.then_inc(conv_evac[k], 1)

            def elu(j, q, l):
                def clip(m):
                    dve.wait_ge(z_mm, zn(j, q, l, m))
                    dve.tensor_scalar(u[:, m, :], pz[:, m, :], n_row[:, l - 1:l] if l else 0.0, 0.0,
                                      ALU.add, ALU.min).then_inc(clip_done, 1)

                def join(m):
                    dve.wait_ge(exp_done, zn(j, q, l, m))
                    dve.scalar_tensor_tensor(out=g[:, m, :], in0=pz[:, m, :], scalar=k_row[:, l - 1:l] if l else 1.0,
                                             in1=u[:, m, :], op0=ALU.add, op1=ALU.max).then_inc(g_written, 1)

                if clips(j):
                    clip(0)
                join(0)
                if clips(j):
                    clip(2)
                for m in range(1, M):
                    join(m)

            def output(j, q):
                dve.wait_ge(out_mm, Q * j + q + 1)
                dve.scalar_tensor_tensor(out=sample(j, q), in0=po[:, :], scalar=n_row[:, 3:4], in1=sample(j, q),
                                         op0=ALU.add, op1=ALU.add).then_inc(out_evac, 1)

            def normal2(i):
                dve.wait_ge(norm_step[2], i * NORM + NORM)
                rows = y2[:, BOX:BOX + K * PITCH].rearrange("p (k w) -> p k w", w=PITCH)[:, :, 0:W]
                dve.tensor_scalar(rows, sample(i).rearrange("p (k w) -> p k w", w=W), st[2][:, 0:1], st[2][:, 1:2],
                                  ALU.mult, ALU.add).then_inc(y2_written, 1)

            def box_scan(i, c):
                if c == 0:
                    dve.wait_ge(y2_written, i + 1)
                rb = rowbox[:, 1:K + 1, :].rearrange("p k w -> p (k w)")
                n = KB * PITCH
                dve.tensor_tensor_scan(rb[:, c * n:(c + 1) * n], y2[:, c * n + BOX:(c + 1) * n + BOX],
                                       y2[:, c * n:(c + 1) * n], 0.0, ALU.add, ALU.subtract).then_inc(box_rows, 1)

            def normal3(i):
                dve.wait_ge(norm_step[3], i * NORM + NORM)
                dve.tensor_scalar(y3[:, :, 1:W + 1], sample(i).rearrange("p (k w) -> p k w", w=W), st[3][:, 0:1],
                                  st[3][:, 1:2], ALU.mult, ALU.add).then_inc(y3_written, 1)

            def near_pairs(i):
                dve.wait_ge(y3_written, i + 1)
                dve.tensor_tensor(pairsum[:, :, :], y3[:, :, 0:W], y3[:, :, 1:W + 1], ALU.add).then_inc(near_rows, 1)

            def near_triples(i):
                dve.wait_ge(near_rows, 2 * i + 1)
                dve.tensor_tensor(rownear[:, 1:K + 1, :], pairsum[:, :, :], y3[:, :, 2:W + 2], ALU.add).then_inc(near_rows, 1)

            def one(t, early, late, mlp, more):
                for p in range(4):
                    conv = work(t, p, early, late)
                    prev = work(t, p - 1, early, late) if p else None
                    for l in range(LAYERS):
                        if mlp:
                            elu(t - 1, p, l)
                        if l == 0 and prev and prev[0] != 3:
                            group_var(prev[1], NEXT[prev[0]])
                        if more:
                            if p == 0 and l < 2:
                                chunk_stats(t + 2, 0, 2 * l)
                                chunk_stats(t + 2, 0, 2 * l + 1)
                                if l == 1:
                                    merge_stats(t + 2, 0)
                            if p == 0 and l == 3:
                                group_var(t + 2, 0)
                            if p == 1 and l == 0:
                                pool_features(t + 2)
                            if p == 1 and l == 2:
                                softmax_in(t + 2)
                            if p == 2 and l == 0:
                                mix(t + 2)
                        if p == 2 and late:
                            if l == 1:
                                normal3(t)
                            if l == 2:
                                near_pairs(t)
                            if l == 3:
                                near_triples(t)
                        if p == 3 and early:
                            if l == 1:
                                normal2(t + 1)
                            if l >= 2:
                                box_scan(t + 1, 2 * l - 4)
                                box_scan(t + 1, 2 * l - 3)
                        if conv:
                            k, i = conv
                            evacuate(i, k, l)
                            if k < 3:
                                chunk_stats(i, k + 1, l)
                    if conv and conv[0] < 3:
                        merge_stats(conv[1], conv[0] + 1)
                    if mlp:
                        output(t - 1, p)

            for c in range(Q):
                chunk_stats(0, 0, c)
            merge_stats(0, 0)
            setup_channels()
            group_var(0, 0)
            pool_features(0)
            softmax_in(0)
            mix(0)
            setup_perceptron()
            rounds(dve, one)


SETUP_DVE = 9 + 9 + 1
N_WEIGHT_DMA = 5 + 4 + 6

_INS = ["x", "L0_conv_w_experts", "L0_conv_bias", "L0_conv_fc_w", "L0_conv_fc_b", "L1_conv_weight",
        "L3_conv_w1", "L3_conv_w2", "L3_conv_w3", "L3_conv_w4", "L3_conv_w5"]


def kernel(**inputs):
    import concourse.bacc as _bacc
    from concourse.bass_utils import run_bass_kernel_spmd as _run

    nc = _bacc.Bacc("TRN2", target_bir_lowering=False, num_devices=1)
    arrays, args = {}, []
    given = {name: np.ascontiguousarray(inputs[name]) for name in _INS}
    given["consts"] = _constants()
    for name, a in given.items():
        arrays[f"in_{name}_dram"] = a
        args.append(nc.dram_tensor(f"in_{name}_dram", a.shape, mybir.dt.from_np(a.dtype), kind="ExternalInput").ap())
    args.append(nc.dram_tensor("out_0_dram", (B, C, H, W), F32, kind="ExternalOutput").ap())
    build(nc, *args)
    r = _run(nc, [arrays], core_ids=[0])
    return r.results[0]["out_0_dram"]
```

```python
from contextlib import ExitStack

import numpy as np

import concourse.bass as bass
from concourse import mybir

F32 = mybir.dt.float32
F32R = mybir.dt.float32r
ALU = mybir.AluOpType
ACT = mybir.ActivationFunctionType
AX = mybir.AxisListType

B, C, H, W = 8, 16, 128, 128
R = 8
K = H // R
P = R * C
N = K * W
Q = 4
KB = K // Q
CH = KB * W
EXPERTS = 3
HID = 64
M = P // 32
BOX = 17
RAD = BOX // 2
PITCH = W + BOX
EPS = 1e-5
HALO = 6 * C
LAYERS = 4

CONSTS = {}


def _constants():
    r, c = np.divmod(np.arange(P), C)
    dr = r[None, :] - r[:, None]
    same = c[None, :] == c[:, None]
    hk = np.arange(P) % (2 * C)
    below, hc = np.divmod(hk, C)
    edge = np.where(below, R - 1, 0)[:, None]
    early = [("group", (c[None, :] // 2 == c[:, None] // 2) / (2 * R)),
             ("neg_group", (c[None, :] // 2 == c[:, None] // 2) / (-2.0 * R)),
             ("chan", same / R),
             ("neg_half", np.full((P, 1), -0.5)),
             ("tap_mask", np.stack([np.arange(R)[None, :] == r[:, None] - kh + 1 for kh in range(3)], 1)),
             ("halo_mask", edge == np.arange(R)[None, :]),
             ("ones", np.ones((P, P)))]
    channel = [("spread", np.arange(C)[:, None] == c[None, :])]
    for n in range(6):
        h = np.arange(HALO)[None, :]
        channel.append((f"spread_halo{n}", (h // C == n) & (h % C == np.arange(C)[:, None])))
    late = [("ident", np.eye(P)), ("one", np.ones((P, 1)))]
    for kh in range(3):
        late.append((f"tap{kh}", same & (dr == 1 - kh)))
    late.append(("halo_tap", (hc[:, None] == c[None, :]) & (edge == r[None, :])))
    late += [("box_above", same & (dr <= 0)), ("box_own", same), ("box_below", same & (dr >= 0))]
    late += [("near_above", same & (dr == 1 - R)), ("near_own", same & (abs(dr) <= 1)),
             ("near_below", same & (dr == R - 1))]
    o = np.arange(P) % HID
    late.append(("fold", (o // 32 * 8 + o % 8)[:, None] == np.arange(C)[None, :]))
    tables = []
    for n, parts in enumerate((early, channel, late)):
        at, cols = 0, []
        for name, m in parts:
            m = np.asarray(m, np.float32)
            m = m.reshape(m.shape[0], -1)
            CONSTS[name] = (n, at, m.shape[1])
            cols.append(m)
            at += m.shape[1]
        tables.append(np.concatenate(cols, axis=1))
    return tables


def build(nc, x, w_experts, conv_bias, fc_w, fc_b, w_depth, w1, w2, w3, w4, w5, con_early, con_channel, con_late, out):
    with ExitStack() as ctx:
        def sb(name, shape, dtype=F32):
            return ctx.enter_context(nc.sbuf_tensor(name, shape, dtype))

        def pb(name, shape):
            return ctx.enter_context(nc.psum_tensor(name, shape, F32))

        def sem(name):
            return ctx.enter_context(nc.semaphore(name))

        def const(name, rows=None):
            table, at, n = CONSTS[name]
            return tables[table][0:rows or tables[table].shape[0], at:at + n]

        xs = sb("xs", [P, B * N])
        y0 = sb("y0", [P, K, W + 2])
        y1 = sb("y1", [P, K, W + 2])
        y2 = sb("y2", [P, K * PITCH + BOX])
        y3 = sb("y3", [P, K, W + 2])
        halo0 = sb("halo0", [HALO, K, W])
        halo1 = sb("halo1", [HALO, K, W])
        box_sum = sb("box_sum", [P, 2, KB * PITCH])
        box_part = [sb(f"box_part{n}", [P, K + 2, W], F32R) for n in range(2)]
        near_sum = box_sum[:, :, :].rearrange("p b n -> p (b n)")[:, 0:2 * CH].rearrange("p (b k w) -> p b k w", k=KB, w=W)
        near_part = [sb(f"near_part{n}", [P, K + 2, W], F32R) for n in range(2)]
        box_mat = sb("box_mat", [P, 3, P], F32R)
        near_mat = sb("near_mat", [P, 3, P], F32R)
        near = sb("near", [P, N])
        near_rest = sb("near_rest", [P, CH], F32R)
        stack = [sb(f"stack{n}", [P, CH], F32R) for n in range(2)]
        u = sb("u", [P, M, CH])
        g = sb("g", [P, M, CH])

        u_flat = u[:, :, :].rearrange("p m n -> p (m n)")
        g_flat = g[:, :, :].rearrange("p m n -> p (m n)")
        con0 = sb("con0", list(con_early.shape))
        NAT = (M + 3) * P
        CHANNEL = con_channel.shape[1]
        LATE = con_late.shape[1]
        wc_in = u_flat[0:C, NAT + CHANNEL:NAT + CHANNEL + EXPERTS * C * 9].rearrange("c (n t) -> c n t", t=9)
        w1raw = g_flat[:, LATE:LATE + P]
        w5raw = g_flat[0:HID, LATE + P:LATE + 2 * P].rearrange("p (a b) -> p a b", b=HID)
        w1eff = g_flat[:, LATE + 2 * P:LATE + 2 * P + C]
        small = g_flat[:, LATE + 2 * P + C:]
        wd_in, bias_in, fcb_in = small[0:C, 0:9], small[0:C, 9:10], small[0:1, 10:10 + EXPERTS]
        tables = [con0[:, :], u_flat[0:C, NAT:NAT + CHANNEL], g_flat[:, 0:LATE]]
        wnat = u_flat[:, 0:NAT].rearrange("p (m n) -> p m n", n=P)

        wc = sb("wc", [P, EXPERTS, C, 9])
        wh = sb("wh", [HALO, EXPERTS, C])
        wmix = sb("wmix", [P, 2, C * 9])
        whmix = sb("whmix", [HALO, 2, C])
        t0 = sb("t0", [P, 3, P])
        tpart = sb("tpart", [P, 3, 3, P])
        th0 = sb("th0", [HALO, P])
        wd = sb("wd", [P, 9])
        wdh = sb("wdh", [HALO, 1])
        t1 = sb("t1", [P, 3, P])
        th1 = sb("th1", [HALO, P])
        bias0 = sb("bias0", [P, 1])
        fcT = sb("fcT", [C, EXPERTS])
        fcb = sb("fcb", [P, EXPERTS])

        w1T = [sb(f"w1T{n}", [P, M, P], F32R) for n in range(2)]
        wT = sb("wT", [P, 3, P])
        w5T = sb("w5T", [P, 32])
        s_row = sb("s_row", [P, 4])
        k_row = sb("k_row", [P, 3])
        n_row = sb("n_row", [P, 4])

        bn = [sb(f"bn{k}", [P, Q, 6]) for k in range(4)]
        ms = [sb(f"ms{k}", [P, 2]) for k in range(4)]
        gs = [sb(f"gs{k}", [P, 4]) for k in range(4)]
        nv = [sb(f"nv{k}", [P, 2]) for k in range(4)]
        st = [sb(f"st{k}", [P, 2]) for k in range(4)]
        pooled = sb("pooled", [C, 1])
        fcp = sb("fcp", [C, EXPERTS])
        logit = sb("logit", [P, EXPERTS])
        nmax = sb("nmax", [P, 1])
        ex = sb("ex", [P, EXPERTS + 1])
        route = sb("route", [P, EXPERTS])

        pz = pb("pz", [P, M, CH])
        pc = pb("pc", [P, 2, CH])
        po = pb("po", [P, CH])
        psm = pb("psm", [P, 512])

        s_early = sem("s_early")
        s_channel = sem("s_channel")
        s_late = sem("s_late")
        s_weights = sem("s_weights")
        x_loaded = sem("x_loaded")
        zeroed = sem("zeroed")
        setup_dve = sem("setup_dve")
        setup_pe = sem("setup_pe")
        setup_pool = sem("setup_pool")
        stat_step = [sem(f"stat_step{k}") for k in range(4)]
        sums_mm = [sem(f"sums_mm{k}") for k in range(4)]
        norm_step = [sem(f"norm_step{k}") for k in range(4)]
        y0_written = sem("y0_written")
        y1_written = sem("y1_written")
        y2_written = sem("y2_written")
        y3_written = sem("y3_written")
        box_rows = sem("box_rows")
        box_high = sem("box_high")
        box_low = sem("box_low")
        near_pairs_done = sem("near_pairs_done")
        near_rows = sem("near_rows")
        near_high = sem("near_high")
        near_low = sem("near_low")
        matrices = sem("matrices")
        near_split = sem("near_split")
        stack_in = sem("stack_in")
        halo0_in = sem("halo0_in")
        halo1_in = sem("halo1_in")
        conv_mm = [sem(f"conv_mm{k}") for k in range(4)]
        conv_evac = [sem(f"conv_evac{k}") for k in range(4)]
        route_step = sem("route_step")
        logits_mm = sem("logits_mm")
        route_exp = sem("route_exp")
        mix_step = sem("mix_step")
        spread_step = sem("spread_step")
        folded = sem("folded")
        z_mm = sem("z_mm")
        relu_done = sem("relu_done")
        clip_done = sem("clip_done")
        exp_done = sem("exp_done")
        g_written = sem("g_written")
        out_mm = sem("out_mm")
        out_evac = sem("out_evac")
        out_stored = sem("out_stored")

        xv = x.rearrange("b c (k r) w -> b r c k w", r=R)
        ov = out.rearrange("b c (k r) w -> b r c k w", r=R)

        def sample(i, j=None):
            if j is None:
                return xs[:, bass.ds(i * N, N)]
            return xs[:, bass.ds(i * N + j * CH, CH)]

        def blocks(t, j):
            return t[:, j * KB:(j + 1) * KB, :]

        def own_rows(t, c):
            return t[:, 1 + c * KB:1 + (c + 1) * KB, :]

        def box_chunk(c):
            return box_sum[:, c % 2, :].rearrange("p (k w) -> p k w", w=PITCH)[:, :, RAD:RAD + W]

        SPLIT = 2
        STACK = 3 * 16
        STAT = Q + 5
        NORM = 2
        ROUTE = 6
        MIX = 6
        SPREAD = 6
        HALO0 = 12 * 16
        HALO1 = 6 * 16
        LOAD = 16

        def zn(j, q, l, m):
            return j * (Q * LAYERS * M) + (q * LAYERS + l) * M + m + 1

        def clips(j, q):
            return (1, 3) if isinstance(j, int) and (j == B - 1 or j == B - 2 and q == 0) else ()

        def carried(j, q):
            return isinstance(j, int) and j == B - 1 and q < Q - 1

        def steps(j, q, l, m, counted):
            n = sum(LAYERS * len(counted(i, p)) for i in range(j + 1) for p in range(Q) if (i, p) < (j, q))
            c = counted(j, q)
            return n + l * len(c) + c.index(m) + 1

        def clip_n(j, q, l, m):
            return steps(j, q, l, m, clips)

        def relu_n(j, q, l, m):
            if not isinstance(j, int):
                return zn(j, q, l, m)
            return steps(j, q, l, m, lambda i, p: [a for a in range(M) if a not in clips(i, p)])

        def apart(j, q):
            return isinstance(j, int) and (j, q) >= (B - 3, Q - 1)

        def elus(j, q, l):
            if l == LAYERS - 1 and apart(j, q):
                return y0[:, :, :].rearrange("p k w -> p (k w)")[:, 0:M * CH].rearrange("p (m n) -> p m n", n=CH)
            return g

        LAYER = (0, 2, 1, 3)
        AHEAD = (1, 0, 1, 0)

        def part_before(t, p):
            if p:
                return t - 1, p - 1
            return None if isinstance(t, int) and t == 1 else (t - 2, Q - 1)

        def norm_at(p, conv, mlp):
            return 1 if p > 1 and conv and not mlp else 0

        NEXT = {0: 1, 1: 2, 2: 3}

        def work(t, p, early, late):
            k, i = LAYER[p], t + AHEAD[p]
            return (k, i) if (early if AHEAD[p] else late) else None

        def before(t, p, early, late):
            if p == 0:
                return None if isinstance(t, int) and t < 0 else (1, 0) if isinstance(t, int) and t == 0 else (3, t - 1)
            for q in range(p - 1, -1, -1):
                if work(t, q, early, late):
                    return work(t, q, early, late)
            return (3, t - 1)

        def rounds(eng, one):
            one(-1, True, False, False, True)
            one(0, True, True, False, True)
            one(1, True, True, True, True)
            with eng.Fori(2, B - 2) as t:
                one(t, True, True, True, True)
            one(B - 2, True, True, True, False)
            one(B - 1, False, True, True, False)
            one(B, False, False, True, False)

        def spread(eng, i):
            eng.wait_ge(mix_step, i * MIX + MIX)
            mixed = wmix[:, 0, :].rearrange("p (o a b) -> p a b o", a=3, b=3)
            mask = const("tap_mask").rearrange("p (a r) -> p a r", a=3)
            for kh in range(3):
                for kw in range(3):
                    ins = eng.tensor_tensor(
                        tpart[:, kh, kw, :].rearrange("p (r o) -> p r o", o=C),
                        mixed[:, kh, kw, :].unsqueeze(1).to_broadcast([P, R, C]),
                        mask[:, kh, :].unsqueeze(2).to_broadcast([P, R, C]), ALU.mult)
                ins.then_inc(spread_step, 1)
            eng.tensor_tensor(th0[:, :].rearrange("p (r o) -> p r o", o=C),
                               whmix[:, 0, :].unsqueeze(1).to_broadcast([HALO, R, C]),
                               const("halo_mask", HALO).unsqueeze(2).to_broadcast([HALO, R, C]), ALU.mult).then_inc(spread_step, 1)
            eng.wait_ge(spread_step, i * SPREAD + 3)
            eng.tensor_tensor(t0[:, :, :], tpart[:, 0, :, :], tpart[:, 1, :, :], ALU.add).then_inc(spread_step, 1)
            eng.wait_ge(spread_step, i * SPREAD + 5)
            eng.tensor_tensor(t0[:, :, :], t0[:, :, :], tpart[:, 2, :, :], ALU.add).then_inc(spread_step, 1)

        block = ctx.enter_context(nc.Block())

        @block.sync
        def _(sp):
            def load(i):
                sp.dma_start(xs[:, bass.ds(i * N, N)].rearrange("p (k w) -> p k w", w=W), xv[i]).then_inc(x_loaded, 16)

            load(0)
            sp.dma_start(tables[0], con_early).then_inc(s_early, 16)
            def halos0(i):
                sp.wait_ge(y0_written, 3 * i + 3)
                for kw in range(3):
                    a, b = kw * 2 * C, (kw * 2 + 1) * C
                    for dst, rows in ((halo0[a:a + C, 1:K], y0[(R - 1) * C:P, 0:K - 1, kw:kw + W]),
                                      (halo0[a:a + C, 0:1], y0[C:2 * C, 0:1, kw:kw + W]),
                                      (halo0[b:b + C, 0:K - 1], y0[0:C, 1:K, kw:kw + W]),
                                      (halo0[b:b + C, K - 1:K], y0[(R - 2) * C:(R - 1) * C, K - 1:K, kw:kw + W])):
                        sp.dma_start(dst, rows).then_inc(halo0_in, 16)

            def halos1(i):
                sp.wait_ge(y1_written, 2 * i + 2)
                for kw in range(3):
                    a, b = kw * 2 * C, (kw * 2 + 1) * C
                    for dst, rows in ((halo1[a:a + C, 1:K], y1[(R - 1) * C:P, 0:K - 1, kw:kw + W]),
                                      (halo1[b:b + C, 0:K - 1], y1[0:C, 1:K, kw:kw + W])):
                        sp.dma_start(dst, rows).then_inc(halo1_in, 16)

            def store(j):
                sp.wait_ge(out_evac, Q * j + Q)
                sp.dma_start(ov[j] if isinstance(j, int) else ov[bass.ds(j, 1)].rearrange("b r c k w -> (b r) c k w"),
                             xs[:, bass.ds(j * N, N)].rearrange("p (k w) -> p k w", w=W)).then_inc(out_stored, 16)

            def stack_rests(j, q):
                sp.wait_ge(near_split, SPLIT * (Q * j + q + 1))
                top, bottom = slice(0, HID), slice(HID, P)

                def move(n, to, source, rows):
                    sp.dma_start(stack[n][to, :].bitcast(F32), source[rows, :].bitcast(F32)).then_inc(stack_in, 16)

                move(1, bottom, stack[0], bottom)
                move(1, top, near_rest, bottom)
                sp.wait_ge(stack_in, STACK * (Q * j + q) + 32)
                move(0, bottom, near_rest, top)

            def one(t, early, late, mlp, more):
                if mlp:
                    stack_rests(t - 1, 1)
                    if not (isinstance(t, int) and t == 1):
                        store(t - 2)
                    stack_rests(t - 1, 2)
                if early:
                    halos1(t + 1)
                if mlp:
                    stack_rests(t - 1, 3)
                if more:
                    halos0(t + 2)
                if late:
                    stack_rests(t, 0)
                if isinstance(t, int) and t < 1:
                    for i in range(2 + 3 * (t + 1), 5 + 3 * (t + 1)):
                        sp.wait_ge(x_loaded, LOAD * i)
                        load(i)

            sp.dma_start(tables[2], con_late).then_inc(s_late, 16)
            halos0(0)
            sp.wait_ge(zeroed, 3)
            sp.wait_ge(x_loaded, LOAD)
            load(1)
            rounds(sp, one)
            store(B - 1)
            sp.wait_ge(out_stored, B * LOAD)

        @block.gpsimd
        def _(pool):
            pool.memset(wnat[:, :, :], 0.0).then_inc(zeroed, 1)
            pool.memset(w5T[:, :], 0.0).then_inc(zeroed, 1)
            pool.memset(halo1[:, :, :], 0.0).then_inc(zeroed, 1)
            for t in (y1, y3):
                pool.memset(t[:, :, 0:1], 0.0).then_inc(zeroed, 1)
                pool.memset(t[:, :, W + 1:W + 2], 0.0).then_inc(zeroed, 1)
            pool.memset(y2[:, :], 0.0).then_inc(zeroed, 1)
            for t in (*box_part, *near_part):
                pool.memset(t[:, 0, :].bitcast(F32), 0.0).then_inc(zeroed, 1)
                pool.memset(t[:, K + 1, :].bitcast(F32), 0.0).then_inc(zeroed, 1)
            pool.wait_ge(zeroed, 16)
            pool.wait_ge(s_early, 16)

            def scales(i, k):
                pool.wait_ge(stat_step[k], i * STAT + STAT)
                pool.tensor_tensor(st[k][:, 0:1], nv[k][:, 1:2], const("neg_half"), ALU.pow).then_inc(norm_step[k], 1)
                pool.wait_ge(norm_step[k], i * NORM + 1)
                pool.tensor_tensor(st[k][:, 1:2], gs[k][:, 2:3], st[k][:, 0:1], ALU.mult).then_inc(norm_step[k], 1)

            def lower_box(i, c):
                pool.wait_ge(box_high, Q * i + c + 1)
                pool.tensor_tensor(own_rows(box_part[1], c), box_chunk(c), own_rows(box_part[0], c), ALU.subtract).then_inc(box_low, 1)

            def lower_near(i, c):
                pool.wait_ge(near_high, Q * i + c + 1)
                pool.tensor_tensor(own_rows(near_part[1], c), near_sum[:, c % 2], own_rows(near_part[0], c), ALU.subtract).then_inc(near_low, 1)

            def split_near(j, q):
                if q > 0:
                    pool.wait_ge(z_mm, zn(j, q - 1, 0, M - 1))
                elif not (isinstance(j, int) and j == 0):
                    pool.wait_ge(z_mm, zn(j - 1, Q - 1, 0, M - 1))
                pool.wait_ge(conv_evac[3], Q * j + q + 1)
                part = near[:, q * CH:(q + 1) * CH]
                pool.tensor_tensor(stack[0][:, :], part, const("ones")[:, 0:1].to_broadcast([P, CH]), ALU.mult).then_inc(near_split, 1)
                pool.wait_ge(near_split, SPLIT * (Q * j + q) + 1)
                pool.tensor_tensor(near_rest[:, :], part, stack[0][:, :], ALU.subtract).then_inc(near_split, 1)

            def one(t, early, late, mlp, more):
                if mlp:
                    split_near(t - 1, 1)
                if late:
                    lower_box(t, 0)
                    lower_box(t, 1)
                    lower_box(t, 2)
                if more:
                    scales(t + 2, 0)
                if early:
                    scales(t + 1, 1)
                if late:
                    lower_box(t, 3)
                if mlp:
                    split_near(t - 1, 2)
                if late:
                    scales(t, 3)
                if mlp:
                    split_near(t - 1, 3)
                if late:
                    for c in range(Q):
                        lower_near(t, c)
                if more:
                    spread(pool, t + 2)
                if early:
                    scales(t + 1, 2)
                if late:
                    split_near(t, 0)

            scales(0, 0)
            rounds(pool, one)

        @block.scalar
        def _(act):
            act.dma_start(tables[1], con_channel).then_inc(s_channel, 16)
            with nc.allow_non_contiguous_dma(reason="small weights, once"):
                act.dma_start(wc_in[:, :, :], w_experts.rearrange("n o c a b -> c (n o) (a b)")).then_inc(s_channel, 16)
                act.dma_start(wd_in[:, :], w_depth.rearrange("c z a b -> c (z a b)")).then_inc(s_channel, 16)
                act.dma_start(bias_in[:, :], conv_bias.rearrange("(c z) -> c z", z=1)).then_inc(s_channel, 16)
                act.dma_start(fcT[:, :], fc_w.rearrange("n c -> c n")).then_inc(s_channel, 16)
            act.dma_start(fcb_in[:, :], fc_b.rearrange("(z n) -> z n", z=1)).then_inc(s_channel, 16)
            for p in range(2):
                act.dma_start(w1raw[p * HID:(p + 1) * HID, :], w1).then_inc(s_weights, 16)
                act.dma_start(w5raw[:, p, :], w5).then_inc(s_weights, 16)
            act.wait_ge(zeroed, 1)
            for p in range(2):
                for l, w in enumerate((w2, w3, w4)):
                    act.dma_start(wnat[p * HID:(p + 1) * HID, M + l, p * HID:(p + 1) * HID], w).then_inc(s_weights, 16)

            def normal0(i):
                act.wait_ge(norm_step[0], i * NORM + NORM)
                act.activation(y0[:, :, 1:W + 1], sample(i).rearrange("p (k w) -> p k w", w=W), ACT.Identity,
                               bias=st[0][:, 1:2], scale=st[0][:, 0:1]).then_inc(y0_written, 1)
                act.wait_ge(y0_written, 3 * i + 1)
                act.copy(y0[:, :, 0:1], y0[:, :, 2:3]).then_inc(y0_written, 1)
                act.copy(y0[:, :, W + 1:W + 2], y0[:, :, W - 1:W]).then_inc(y0_written, 1)

            def normal1(i, half):
                act.wait_ge(norm_step[1], i * NORM + NORM)
                rows = slice(half * K // 2, (half + 1) * K // 2)
                act.activation(y1[:, rows, 1:W + 1], sample(i).rearrange("p (k w) -> p k w", w=W)[:, rows, :], ACT.Abs,
                               bias=st[1][:, 1:2], scale=st[1][:, 0:1]).then_inc(y1_written, 1)

            def round_box(i, c):
                act.wait_ge(box_rows, Q * i + c + 1)
                if c == 0 and not (isinstance(i, int) and i == 0):
                    act.wait_ge(conv_mm[2], Q * i)
                act.copy(own_rows(box_part[0], c), box_chunk(c)).then_inc(box_high, 1)

            def round_near(i, c):
                act.wait_ge(near_rows, Q * i + c + 1)
                if c == 0 and not (isinstance(i, int) and i == 0):
                    act.wait_ge(conv_mm[3], Q * i)
                act.copy(own_rows(near_part[0], c), near_sum[:, c % 2]).then_inc(near_high, 1)

            def softmax_exp(i):
                act.wait_ge(route_step, i * ROUTE + 4)
                act.activation(ex[:, 0:EXPERTS], logit[:, :], ACT.Exp, bias=nmax[:, 0:1],
                               accum_out=ex[:, EXPERTS:EXPERTS + 1]).then_inc(route_exp, 1)

            def elu(j, q, l):
                def relu(m):
                    act.wait_ge(z_mm, zn(j, q, l, m))
                    act.activation(u[:, m, :], pz[:, m, :], ACT.Relu, scale=-1.0,
                                   bias=s_row[:, l - 1:l] if l else 0.0).then_inc(relu_done, 1)

                def exp(m):
                    if m in clips(j, q):
                        act.wait_ge(clip_done, clip_n(j, q, l, m))
                        act.activation(u[:, m, :], u[:, m, :], ACT.Exp).then_inc(exp_done, 1)
                    else:
                        act.wait_ge(relu_done, relu_n(j, q, l, m))
                        act.activation(u[:, m, :], u[:, m, :], ACT.Exp, scale=-1.0).then_inc(exp_done, 1)

                if clips(j, q):
                    relu(0)
                    exp(0)
                    exp(1)
                    relu(2)
                    exp(2)
                    exp(3)
                else:
                    relu(0)
                    for m in range(1, M):
                        relu(m)
                        exp(m - 1)
                    exp(M - 1)

            def one(t, early, late, mlp, more):
                for p in range(4):
                    for l in range(LAYERS):
                        if mlp:
                            elu(t - 1, p, l)
                        if p == 0 and l > 0 and late:
                            round_box(t, l - 1)
                        if p == 1 and l == 0 and late:
                            round_box(t, 3)
                        if p == 1 and l in (1, 3) and early:
                            normal1(t + 1, 0 if l == 1 else 1)
                        if p == 1 and l == 3 and more:
                            softmax_exp(t + 2)
                        if p == 2 and l == 0 and more:
                            normal0(t + 2)
                        if p == 2 and l >= 2 and late:
                            round_near(t, 2 * l - 4)
                            round_near(t, 2 * l - 3)

            normal0(0)
            softmax_exp(0)
            rounds(act, one)

        @block.tensor
        def _(pe):
            def group_sums(i, k):
                pe.wait_ge(stat_step[k], i * STAT + Q + 2)
                pe.matmul(psm[:, 0:2], const("group"), ms[k][:, :], start=True, stop=True)
                last = pe.matmul(psm[:, 2:3], const("neg_group"), ms[k][:, 0:1], start=True, stop=True)
                if k == 0:
                    last = pe.matmul(psm[:, 3:4], const("chan"), ms[k][:, 0:1], start=True, stop=True)
                last.then_inc(sums_mm[k], 1)

            def logits(i):
                pe.wait_ge(route_step, i * ROUTE + 2)
                pe.matmul(psm[:, 8:8 + EXPERTS], const("ones", C), fcp[:, :], start=True, stop=True).then_inc(logits_mm, 1)

            def banded(o, mats, parts, j):
                for d in range(3):
                    for n in range(2):
                        last = pe.matmul(o, mats[:, d, :], parts[n][:, j * KB + d:(j + 1) * KB + d, :],
                                         start=d == 0 and n == 0, stop=d == 2 and n == 1)
                return last

            def conv_chunk(i, k, j, last_conv):
                o = pc[:, j % 2, :]
                if j >= 2:
                    pe.wait_ge(conv_evac[k], Q * i + j - 1)
                elif last_conv:
                    pe.wait_ge(conv_evac[last_conv[0]], Q * last_conv[1] + j + 3)
                if k == 0:
                    if j == 0:
                        pe.wait_ge(y0_written, 3 * i + 3)
                        pe.wait_ge(spread_step, SPREAD * i + SPREAD)
                    for kw in range(3):
                        pe.matmul(o, t0[:, kw, :], blocks(y0, j)[:, :, kw:kw + W], start=kw == 0, stop=False)
                    if j == 0:
                        pe.wait_ge(halo0_in, HALO0 * i + HALO0)
                    last = pe.matmul(o, th0[:, :], blocks(halo0, j), start=False, stop=True)
                elif k == 1:
                    if j == 0:
                        if isinstance(i, int) and i == 0:
                            pe.wait_ge(setup_dve, SETUP_DVE)
                        pe.wait_ge(y1_written, 2 * i + 2)
                    for kw in range(3):
                        pe.matmul(o, t1[:, kw, :], blocks(y1, j)[:, :, kw:kw + W], start=kw == 0, stop=False)
                    if j == 0:
                        pe.wait_ge(halo1_in, HALO1 * i + HALO1)
                    last = pe.matmul(o, th1[:, :], blocks(halo1, j), start=False, stop=True)
                elif k == 2:
                    pe.wait_ge(box_low, Q * i + min(j + 2, Q))
                    if isinstance(i, int) and i == 0 and j == 0:
                        pe.wait_ge(matrices, 3)
                    last = banded(o, box_mat, box_part, j)
                else:
                    pe.wait_ge(near_low, Q * i + min(j + 2, Q))
                    if isinstance(i, int) and i == 0 and j == 0:
                        pe.wait_ge(matrices, 4)
                    last = banded(o, near_mat, near_part, j)
                last.then_inc(conv_mm[k], 1)

            def layer(j, q, l):
                for m in range(M):
                    if l == 0:
                        if q > 0:
                            pe.wait_ge(g_written, zn(j, q - 1, LAYERS - 1, m))
                        elif not (isinstance(j, int) and j == 0):
                            pe.wait_ge(g_written, zn(j - 1, Q - 1, LAYERS - 1, m))
                        if m == 0:
                            pe.wait_ge(stack_in, STACK * (Q * j + q + 1))
                        for n in range(2):
                            last = pe.matmul(pz[:, m, :], w1T[n][:, m, :], stack[m // 2][:, :], start=n == 0, stop=n == 1)
                        last.then_inc(z_mm, 1)
                    else:
                        pe.wait_ge(g_written, zn(j, q, l - 1, m))
                        pe.matmul(pz[:, m, :], wT[:, l - 1, :], g[:, m, :],
                                  start=True, stop=True).then_inc(z_mm, 1)

            def last_layer(j, q):
                pe.wait_ge(g_written, zn(j, q, LAYERS - 1, M - 1))
                for m in range(M):
                    last = pe.matmul(po[32 * m:32 * m + 32, :], w5T[:, :], elus(j, q, LAYERS - 1)[:, m, :],
                                     start=True, stop=True)
                last.then_inc(out_mm, 1)

            def one(t, early, late, mlp, more):
                for p in range(4):
                    conv = work(t, p, early, late)
                    prev = work(t, p - 1, early, late) if p else None
                    for l in range(LAYERS):
                        if mlp:
                            layer(t - 1, p, l)
                            if l == 0 and part_before(t, p):
                                last_layer(*part_before(t, p))
                        if l == norm_at(p, conv, mlp) and prev and prev[0] != 3:
                            group_sums(prev[1], NEXT[prev[0]])
                        if p == 0 and l == 3 and more:
                            group_sums(t + 2, 0)
                        if p == 1 and l == 1 and more:
                            logits(t + 2)
                        if conv:
                            conv_chunk(conv[1], conv[0], l, before(t, p, early, late))

            def spread_channels():
                pe.wait_ge(s_channel, 16 * N_CHANNEL_DMA)
                pe.matmul(pc[:, 0, 0:EXPERTS * C * 9], const("spread", C), wc_in[:, :, :].rearrange("c n t -> c (n t)"),
                          start=True, stop=True)
                pe.matmul(pc[:, 0, 500:509], const("spread", C), wd_in[:, :], start=True, stop=True)
                pe.matmul(pc[:, 0, 510:511], const("spread", C), bias_in[:, :], start=True, stop=True)
                pe.matmul(pc[:, 0, 440:440 + EXPERTS], const("ones", 1), fcb_in[:, :], start=True, stop=True)
                taps = [2 * below * 3 + kw for kw in range(3) for below in range(2)]
                for n, tap in enumerate(taps):
                    pe.matmul(pc[0:HALO, 1, 0:EXPERTS * C], const(f"spread_halo{n}", C), wc_in[:, :, tap], start=n == 0, stop=n == 5)
                for n, tap in enumerate(taps):
                    last = pe.matmul(pc[0:HALO, 1, 100:101], const(f"spread_halo{n}", C), wd_in[:, tap:tap + 1], start=n == 0, stop=n == 5)
                last.then_inc(setup_pe, 1)

            pe.wait_ge(s_early, 16)
            group_sums(0, 0)
            spread_channels()
            pe.wait_ge(s_late, 16)
            pe.wait_ge(setup_dve, 2)
            for n in range(M + 3):
                last = pe.transpose(pz[:, :, :].rearrange("p a n -> p (a n)")[:, n * P:(n + 1) * P], wnat[:, n, :], const("ident"))
            last.then_inc(setup_pe, 1)
            pe.matmul(po[:, 16:16 + C], w5raw[:, :, :].rearrange("k p c -> k (p c)"), const("fold", HID),
                      start=True, stop=True).then_inc(setup_pe, 1)
            logits(0)
            pe.wait_ge(setup_dve, 6)
            for l in range(3):
                pe.matmul(po[:, 64 + l:65 + l], wT[:, l, :], const("one"), start=True, stop=True)
            for m in range(M):
                last = pe.matmul(po[32 * m:32 * m + 32, 67:68], w5T[:, :], const("one"), start=True, stop=True)
            last.then_inc(setup_pe, 1)
            rounds(pe, one)
            last_layer(B - 1, Q - 1)

        @block.vector
        def _(dve):
            def setup_natural():
                dve.wait_ge(s_weights, 16 * N_WEIGHT_DMA)
                dve.wait_ge(zeroed, 2)
                dve.tensor_reduce(w1eff[:, :], w1raw[:, :].rearrange("p (c e) -> p c e", e=8), AX.X, ALU.add).then_inc(setup_dve, 1)
                dve.wait_ge(setup_dve, 1)
                for m in range(M):
                    for p in range(2):
                        for at in range(p * C + m % 2 * 2 * C, P, HID):
                            last = dve.tensor_copy(wnat[p * HID:(p + 1) * HID, m, at:at + C], w1eff[p * HID:(p + 1) * HID, :])
                last.then_inc(setup_dve, 1)

            def setup_channels():
                dve.wait_ge(setup_pe, 1)
                dve.tensor_copy(wc[:, :, :, :].rearrange("p n o t -> p (n o t)"), pc[:, 0, 0:EXPERTS * C * 9])
                dve.tensor_copy(wd[:, :], pc[:, 0, 500:509])
                dve.tensor_copy(bias0[:, :], pc[:, 0, 510:511])
                dve.tensor_copy(fcb[:, :], pc[:, 0, 440:440 + EXPERTS])
                dve.tensor_copy(wh[:, :, :].rearrange("p n o -> p (n o)"), pc[0:HALO, 1, 0:EXPERTS * C])
                dve.tensor_copy(wdh[:, :], pc[0:HALO, 1, 100:101]).then_inc(setup_dve, 1)

            def setup_transposed():
                dve.wait_ge(setup_pe, 2)
                turned = pz[:, :, :].rearrange("p a n -> p (a n)")[:, 0:(M + 3) * P].rearrange("p (m n) -> p m n", n=P)
                dve.tensor_copy(w1T[0][:, :, :], turned[:, 0:M, :]).then_inc(matrices, 1)
                dve.tensor_copy(wT[:, :, :], turned[:, M:, :]).then_inc(setup_dve, 1)
                dve.wait_ge(matrices, 1)
                dve.tensor_tensor(w1T[1][:, :, :], turned[:, 0:M, :], w1T[0][:, :, :], ALU.subtract).then_inc(matrices, 1)
                dve.wait_ge(setup_pe, 3)
                for p in range(2):
                    dve.tensor_scalar(w5T[p * HID:(p + 1) * HID, p * C:(p + 1) * C], po[p * HID:(p + 1) * HID, 16:16 + C],
                                      0.025, None, ALU.mult).then_inc(setup_dve, 1)

            def setup_depthwise():
                dve.wait_ge(setup_pe, 4)
                dve.tensor_copy(s_row[:, :], po[:, 64:68]).then_inc(setup_dve, 1)
                dve.wait_ge(setup_dve, 7)
                dve.tensor_scalar(k_row[:, 0:3], s_row[:, 0:3], -1.0, 1.0, ALU.mult, ALU.add).then_inc(setup_dve, 1)
                dve.tensor_scalar(n_row[:, :], s_row[:, :], -1.0, None, ALU.mult).then_inc(setup_dve, 1)
                dve.wait_ge(s_late, 16)
                for kh in range(3):
                    for kw in range(3):
                        if kh:
                            dve.wait_ge(setup_dve, 7 + 3 * kh + kw)
                            dve.scalar_tensor_tensor(out=t1[:, kw, :], in0=const(f"tap{kh}"), scalar=wd[:, 3 * kh + kw:3 * kh + kw + 1],
                                                     in1=t1[:, kw, :], op0=ALU.mult, op1=ALU.add).then_inc(setup_dve, 1)
                        else:
                            dve.tensor_scalar(t1[:, kw, :], const("tap0"), wd[:, kw:kw + 1], None, ALU.mult).then_inc(setup_dve, 1)
                dve.tensor_scalar(th1[:, :], const("halo_tap", HALO), wdh[:, 0:1], None, ALU.mult).then_inc(setup_dve, 1)

            def chunk_stats(i, k, c):
                if k == 0:
                    if c == 0:
                        dve.wait_ge(x_loaded, LOAD * i + LOAD)
                else:
                    dve.wait_ge(conv_evac[k - 1], Q * i + c + 1)
                dve.nop(nofuse=True)
                dve.bn_stats(bn[k][:, c, :], sample(i, c)).then_inc(stat_step[k], 1)

            def merge_stats(i, k):
                dve.wait_ge(stat_step[k], i * STAT + Q)
                dve.nop(nofuse=True)
                dve.bn_aggr(ms[k][:, :], bn[k][:, :, :].rearrange("p q s -> p (q s)")).then_inc(stat_step[k], 1)
                dve.wait_ge(stat_step[k], i * STAT + Q + 1)
                dve.scalar_tensor_tensor(out=ms[k][:, 1:2], in0=ms[k][:, 0:1], scalar=ms[k][:, 0:1], in1=ms[k][:, 1:2],
                                         op0=ALU.mult, op1=ALU.add).then_inc(stat_step[k], 1)

            def group_var(i, k):
                n = 4 if k == 0 else 3
                dve.wait_ge(sums_mm[k], i + 1)
                dve.tensor_copy(gs[k][:, 0:n], psm[:, 0:n]).then_inc(stat_step[k], 1)
                dve.wait_ge(stat_step[k], i * STAT + Q + 3)
                dve.scalar_tensor_tensor(out=nv[k][:, 0:1], in0=gs[k][:, 0:1], scalar=gs[k][:, 0:1], in1=gs[k][:, 1:2],
                                         op0=ALU.mult, op1=ALU.subtract).then_inc(stat_step[k], 1)
                dve.wait_ge(stat_step[k], i * STAT + Q + 4)
                dve.tensor_scalar(nv[k][:, 1:2], nv[k][:, 0:1], -1.0, EPS, ALU.mult, ALU.add).then_inc(stat_step[k], 1)

            def pool_features(i):
                dve.wait_ge(norm_step[0], i * NORM + NORM)
                dve.tensor_scalar(pooled[:, :], gs[0][0:C, 3:4], st[0][0:C, 0:1], st[0][0:C, 1:2], ALU.mult, ALU.add).then_inc(route_step, 1)
                dve.wait_ge(route_step, i * ROUTE + 1)
                dve.tensor_scalar(fcp[:, :], fcT[:, :], pooled[:, 0:1], None, ALU.mult).then_inc(route_step, 1)

            def softmax_in(i):
                dve.wait_ge(logits_mm, i + 1)
                dve.tensor_tensor(logit[:, :], psm[:, 8:8 + EXPERTS], fcb[:, :], ALU.add).then_inc(route_step, 1)
                dve.wait_ge(route_step, i * ROUTE + 3)
                dve.tensor_reduce(nmax[:, :], logit[:, :], AX.X, ALU.max, negate=True).then_inc(route_step, 1)

            def mix(i):
                n = MIX * i
                dve.wait_ge(route_exp, i + 1)
                dve.reciprocal(nmax[:, :], ex[:, EXPERTS:EXPERTS + 1]).then_inc(route_step, 1)
                dve.wait_ge(route_step, i * ROUTE + 5)
                dve.tensor_scalar(route[:, :], ex[:, 0:EXPERTS], nmax[:, 0:1], None, ALU.mult).then_inc(route_step, 1)
                dve.wait_ge(route_step, i * ROUTE + 6)
                src = [wc[:, e, :, :].rearrange("p o t -> p (o t)") for e in range(EXPERTS)]
                srch = [wh[:, e, :] for e in range(EXPERTS)]
                dve.tensor_scalar(wmix[:, 0, :], src[0], route[:, 0:1], None, ALU.mult).then_inc(mix_step, 1)
                dve.tensor_scalar(whmix[:, 0, :], srch[0], route[0:HALO, 0:1], None, ALU.mult).then_inc(mix_step, 1)
                for e in range(1, EXPERTS):
                    dve.wait_ge(mix_step, n + 2 * e)
                    dve.scalar_tensor_tensor(out=wmix[:, e % 2, :], in0=src[e], scalar=route[:, e:e + 1],
                                             in1=wmix[:, (e + 1) % 2, :], op0=ALU.mult, op1=ALU.add).then_inc(mix_step, 1)
                    dve.scalar_tensor_tensor(out=whmix[:, e % 2, :], in0=srch[e], scalar=route[0:HALO, e:e + 1],
                                             in1=whmix[:, (e + 1) % 2, :], op0=ALU.mult, op1=ALU.add).then_inc(mix_step, 1)

            def evacuate(i, k, c):
                dve.wait_ge(conv_mm[k], Q * i + c + 1)
                o = pc[:, c % 2, :]
                if k == 0:
                    ins = dve.scalar_tensor_tensor(out=sample(i, c), in0=o, scalar=bias0[:, 0:1], in1=sample(i, c),
                                                   op0=ALU.add, op1=ALU.add)
                elif k == 1:
                    ins = dve.tensor_tensor(sample(i, c), o, sample(i, c), ALU.add)
                elif k == 2:
                    ins = dve.scalar_tensor_tensor(out=sample(i, c), in0=o, scalar=1.0 / (BOX * BOX), in1=sample(i, c),
                                                   op0=ALU.mult, op1=ALU.add)
                else:
                    ins = dve.tensor_tensor(near[:, c * CH:(c + 1) * CH].rearrange("p (k w) -> p k w", w=W),
                                            o.rearrange("p (k w) -> p k w", w=W), blocks(y3, c)[:, :, 1:W + 1], ALU.subtract)
                ins.then_inc(conv_evac[k], 1)

            def elu(j, q, l):
                def clip(m):
                    dve.wait_ge(z_mm, zn(j, q, l, m))
                    dve.tensor_scalar(u[:, m, :], pz[:, m, :], n_row[:, l - 1:l] if l else 0.0, 0.0,
                                      ALU.add, ALU.min).then_inc(clip_done, 1)

                def join(l, m, q=q):
                    dve.wait_ge(exp_done, zn(j, q, l, m))
                    dve.scalar_tensor_tensor(out=elus(j, q, l)[:, m, :], in0=pz[:, m, :], scalar=k_row[:, l - 1:l] if l else 1.0,
                                             in1=u[:, m, :], op0=ALU.add, op1=ALU.max).then_inc(g_written, 1)

                if not clips(j, q):
                    for m in range(M):
                        join(l, m)
                    return
                if l > 0:
                    join(l - 1, 3)
                elif q > 0 and carried(j, q - 1):
                    join(LAYERS - 1, 3, q - 1)
                clip(1)
                join(l, 0)
                join(l, 1)
                clip(3)
                join(l, 2)
                if l == LAYERS - 1 and not carried(j, q):
                    join(l, 3)

            def output(j, q):
                dve.wait_ge(out_mm, Q * j + q + 1)
                dve.scalar_tensor_tensor(out=sample(j, q), in0=po[:, :], scalar=n_row[:, 3:4], in1=sample(j, q),
                                         op0=ALU.add, op1=ALU.add).then_inc(out_evac, 1)

            def normal2(i):
                dve.wait_ge(norm_step[2], i * NORM + NORM)
                rows = y2[:, BOX:BOX + K * PITCH].rearrange("p (k w) -> p k w", w=PITCH)[:, :, 0:W]
                dve.tensor_scalar(rows, sample(i).rearrange("p (k w) -> p k w", w=W), st[2][:, 0:1], st[2][:, 1:2],
                                  ALU.mult, ALU.add).then_inc(y2_written, 1)

            def box_scan(i, c):
                if c == 0:
                    dve.wait_ge(y2_written, i + 1)
                if c >= 2:
                    dve.wait_ge(box_low, Q * i + c - 1)
                n = KB * PITCH
                dve.tensor_tensor_scan(box_sum[:, c % 2, :], y2[:, c * n + BOX:(c + 1) * n + BOX],
                                       y2[:, c * n:(c + 1) * n], 0.0, ALU.add, ALU.subtract).then_inc(box_rows, 1)

            def normal3(i):
                dve.wait_ge(norm_step[3], i * NORM + NORM)
                dve.tensor_scalar(y3[:, :, 1:W + 1], sample(i).rearrange("p (k w) -> p k w", w=W), st[3][:, 0:1],
                                  st[3][:, 1:2], ALU.mult, ALU.add).then_inc(y3_written, 1)

            def near_sums(i, c):
                if c == 0:
                    dve.wait_ge(y3_written, i + 1)
                if c >= 2:
                    dve.wait_ge(near_low, Q * i + c - 1)
                y = blocks(y3, c)
                dve.tensor_tensor(near_sum[:, c % 2], y[:, :, 0:W], y[:, :, 1:W + 1], ALU.add).then_inc(near_pairs_done, 1)
                dve.wait_ge(near_pairs_done, Q * i + c + 1)
                dve.tensor_tensor(near_sum[:, c % 2], near_sum[:, c % 2], y[:, :, 2:W + 2], ALU.add).then_inc(near_rows, 1)

            def one(t, early, late, mlp, more):
                for p in range(4):
                    conv = work(t, p, early, late)
                    prev = work(t, p - 1, early, late) if p else None
                    for l in range(LAYERS):
                        if mlp:
                            last = part_before(t, p) if l == 0 else None
                            if last and not apart(*last):
                                output(*last)
                            elu(t - 1, p, l)
                            if last and apart(*last):
                                output(*last)
                        if l == norm_at(p, conv, mlp) and prev and prev[0] != 3:
                            group_var(prev[1], NEXT[prev[0]])
                        if p == 0 and late:
                            box_scan(t, l)
                        if more:
                            if p == 0 and l < 3:
                                for c in ((0,), (1, 2), (3,))[l]:
                                    chunk_stats(t + 2, 0, c)
                                if l == 2:
                                    merge_stats(t + 2, 0)
                            if p == 0 and l == 3:
                                group_var(t + 2, 0)
                            if p == 1 and l == 0:
                                pool_features(t + 2)
                            if p == 1 and l == 2:
                                softmax_in(t + 2)
                            if p == 2 and l == 0:
                                mix(t + 2)
                        if p == 2 and late:
                            if l == 1:
                                normal3(t)
                                near_sums(t, 0)
                                near_sums(t, 1)
                            if l == 2:
                                near_sums(t, 2)
                            if l == 3:
                                near_sums(t, 3)
                        if p == 3 and early:
                            if l == 1:
                                normal2(t + 1)
                        if conv:
                            k, i = conv
                            evacuate(i, k, l)
                            if k < 3:
                                chunk_stats(i, k + 1, l)
                    if conv and conv[0] < 3:
                        merge_stats(conv[1], conv[0] + 1)

            for c in range(Q):
                chunk_stats(0, 0, c)
            merge_stats(0, 0)
            group_var(0, 0)
            setup_natural()
            setup_channels()
            pool_features(0)
            setup_transposed()
            softmax_in(0)
            mix(0)
            spread(dve, 0)
            setup_depthwise()
            for d, side in enumerate(("above", "own", "below")):
                last = dve.tensor_copy(box_mat[:, d, :], const(f"box_{side}"))
            last.then_inc(matrices, 1)
            for d, side in enumerate(("above", "own", "below")):
                last = dve.tensor_copy(near_mat[:, d, :], const(f"near_{side}"))
            last.then_inc(matrices, 1)
            rounds(dve, one)
            output(B - 1, Q - 1)


SETUP_DVE = 9 + 9 + 1
N_CHANNEL_DMA = 6
N_WEIGHT_DMA = 4 + 6

_INS = ["x", "L0_conv_w_experts", "L0_conv_bias", "L0_conv_fc_w", "L0_conv_fc_b", "L1_conv_weight",
        "L3_conv_w1", "L3_conv_w2", "L3_conv_w3", "L3_conv_w4", "L3_conv_w5"]


def kernel(**inputs):
    import concourse.bacc as _bacc
    from concourse.bass_utils import run_bass_kernel_spmd as _run

    nc = _bacc.Bacc("TRN2", target_bir_lowering=False, num_devices=1)
    arrays, args = {}, []
    given = {name: np.ascontiguousarray(inputs[name]) for name in _INS}
    given["con_early"], given["con_channel"], given["con_late"] = _constants()
    for name, a in given.items():
        arrays[f"in_{name}_dram"] = a
        args.append(nc.dram_tensor(f"in_{name}_dram", a.shape, mybir.dt.from_np(a.dtype), kind="ExternalInput").ap())
    args.append(nc.dram_tensor("out_0_dram", (B, C, H, W), F32, kind="ExternalOutput").ap())
    build(nc, *args)
    r = _run(nc, [arrays], core_ids=[0])
    return r.results[0]["out_0_dram"]
```
